# Optimizing a Trainium2 kernel written in Bass

```python
import numpy as np
import jax
import jax.numpy as jnp

def _softmax(x, axis=-1):
    return jax.nn.softmax(x, axis=axis)

def _gelu(x):
    return jax.nn.gelu(x, approximate=True)

def _silu(x):
    return jax.nn.silu(x)

def _sigmoid(x):
    return jax.nn.sigmoid(x)

def _layernorm(x, axis=-1, eps=1e-05):
    m = jnp.mean(x, axis=axis, keepdims=True)
    v = jnp.var(x, axis=axis, keepdims=True)
    return (x - m) / jnp.sqrt(v + eps)

def _scatter_add(tgt, idx, src, axis=0):
    return tgt.at[idx].add(src)

def _segment_sum(src, seg, n):
    return jax.ops.segment_sum(src, seg, n)
kernel_name = 'mk_flamingo_gated_d1_seqx_r8_87c24e'

def setup_inputs(seed: int=0):
    np.random.seed(seed)
    _w = jnp.asarray

    def _rec_inputs():
        import jax
        import jax.numpy as jnp
        _rk = jax.random.key(seed)
        x = -0.0003929 + 0.9999 * jax.random.normal(jax.random.fold_in(_rk, 1), (4, 512, 128), jnp.float32)
        _lenS = 512 - jax.random.randint(jax.random.fold_in(_rk, 7), (4,), 0, max(1, 512 // 4) + 1, jnp.int32)
        _lenS2 = 77 - jax.random.randint(jax.random.fold_in(_rk, 8), (4,), 0, max(1, 77 // 4) + 1, jnp.int32)
        _ctx_2048P = jax.random.normal(jax.random.fold_in(_rk, 11), (4, 16, 256), jnp.float32)
        _ctx_2048c = jax.random.dirichlet(jax.random.fold_in(_rk, 511), 0.3 * jnp.ones((16,), jnp.float32), (4, 77))
        _ctx_2048t = jnp.einsum('bsk,bkd->bsd', _ctx_2048c, _ctx_2048P)
        _ctx_2048t = _ctx_2048t * jax.lax.rsqrt(jnp.mean(jnp.square(_ctx_2048t)) + 1e-12) * 0.953939
        ctx_2048 = 4.13588e-05 + 0.999923 * (_ctx_2048t + 0.3 * jax.random.normal(jax.random.fold_in(_rk, 611), (4, 77, 256), jnp.float32))
        _validS = jnp.arange(512)[None, :] < _lenS[:, None]
        _validS2 = jnp.arange(77)[None, :] < _lenS2[:, None]
        _causal = jnp.tril(jnp.ones((512, 512), dtype=bool))
        mask_BxS2_if0 = jnp.where(jnp.ones((4, 77), dtype=bool), 4, 0).astype(jnp.int32)
        _g = jax.random.normal(jax.random.fold_in(_rk, 9001), (2, 1), jnp.float32)
        _g = jnp.sign(_g) * jnp.maximum(jnp.abs(_g), 1.0) + (_g == 0) * 1.0
        g_xattn = _g[0]
        g_ffn = _g[1]
        return (x, ctx_2048, mask_BxS2_if0, g_xattn, g_ffn)
    x, ctx_2048, mask_BxS2_if0, g_xattn, g_ffn = _rec_inputs()

    def _L0_xattn_setup():
        import jax, jax.numpy as jnp
        import numpy as np
        B, L, P = (4, 512, 128)
        D_MODEL = 128
        D_GLOBAL = 256
        HEADDIM = 32
        EPSILON = 0.001
        RMS_EPS = 1e-05

        def rmsnorm(x, g, eps=RMS_EPS):
            var = jnp.mean(jnp.square(x), axis=-1, keepdims=True)
            return x * jax.lax.rsqrt(var + eps) * g

        def _hnet_depool(h, h_patch_full, patch_lens):
            h_patch = h_patch_full[..., :D_MODEL]
            bsz, plen = (h_patch.shape[0], h_patch.shape[1])
            seqlen = h.shape[1]
            logp = jnp.full((bsz, plen), -EPSILON, dtype=jnp.float32)
            bidx = jnp.cumsum(patch_lens, axis=1) - 1
            boundary_mask = jnp.zeros((bsz, seqlen), dtype=jnp.int32)
            boundary_mask = boundary_mask.at[jnp.arange(bsz)[:, None], bidx].set(1)
            dt = (-jnp.log(-jnp.expm1(logp))).astype(h_patch.dtype)
            x = h_patch / dt[..., None]
            n_heads = D_MODEL // HEADDIM
            A = -jnp.ones((n_heads,), dtype=jnp.float32)
            bcoef = jnp.exp(logp).astype(h_patch.dtype)
            x4 = x.reshape(bsz, plen, n_heads, HEADDIM)
            a = jnp.exp(dt[:, :, None] * A[None, None, :])
            u = (dt * bcoef)[:, :, None, None] * x4
            a_b = jnp.broadcast_to(a[..., None], u.shape)

            def comb(lft, rgt):
                aL, uL = lft
                aR, uR = rgt
                return (aL * aR, uL * aR + uR)
            _, s = jax.lax.associative_scan(comb, (a_b, u), axis=1)
            depool = s.reshape(bsz, plen, D_MODEL)
            plug = jnp.clip(jnp.cumsum(boundary_mask, axis=1) - 1, 0, plen - 1)
            depool_out = depool[jnp.arange(bsz)[:, None], plug]
            return depool_out + h
        key = jax.random.key(seed)
        k1, k2, k3, k4 = jax.random.split(key, 4)
        embeds = jax.random.normal(k1, (B, L, D_MODEL), dtype=jnp.float32)
        patch_embeds = jax.random.normal(k2, (B, P, D_GLOBAL), dtype=jnp.float32)
        patch_lens = jnp.full((B, P), L // P, dtype=jnp.int64)
        W_in = jax.random.normal(k3, (D_MODEL, D_MODEL), dtype=jnp.float32) * 0.02
        b_in = jnp.zeros((D_MODEL,), dtype=jnp.float32)
        g_res = jnp.ones((D_MODEL,), dtype=jnp.float32)
        g_init = jnp.ones((D_GLOBAL,), dtype=jnp.float32)
        return {'embeds': embeds, 'patch_embeds': patch_embeds, 'patch_lens': patch_lens, 'W_in': W_in, 'b_in': b_in, 'g_res': g_res, 'g_init': g_init}
    _L0_xattn_all = _L0_xattn_setup()
    _L0_xattn_in = {k: v for k, v in _L0_xattn_all.items() if k in ('W_in', 'b_in', 'g_res', 'g_init')}
    del _L0_xattn_all

    def _L0_ffn_setup():
        import jax, jax.numpy as jnp
        import numpy as np
        B, SEQ, DIM = (2, 512, 128)
        E, S = (8, 64)
        HID = 4 * DIM
        SCALE = DIM ** 0.5

        def rmsnorm(x, gamma):
            n = jnp.linalg.norm(x, axis=-1, keepdims=True)
            return x / jnp.maximum(n, 1e-12) * SCALE * gamma
        key = jax.random.key(seed)
        ks = jax.random.split(key, 4)
        w_init = lambda k, shape: jax.random.normal(k, shape, dtype=jnp.float32) * 0.02
        return {'x': jax.random.normal(ks[0], (B, SEQ, DIM), dtype=jnp.float32), 'norm_gamma': jnp.ones((DIM,), jnp.float32), 'slot_norm_gamma': jnp.ones((DIM,), jnp.float32), 'slot_embeds': jax.random.normal(ks[1], (E, S, DIM), dtype=jnp.float32), 'w1': w_init(ks[2], (E, DIM, HID)), 'b1': jnp.zeros((E, HID), jnp.float32), 'w2': w_init(ks[3], (E, HID, DIM)), 'b2': jnp.zeros((E, DIM), jnp.float32)}
    _L0_ffn_all = _L0_ffn_setup()
    _L0_ffn_in = {k: v for k, v in _L0_ffn_all.items() if k in ('norm_gamma', 'slot_norm_gamma', 'slot_embeds', 'w1', 'b1', 'w2', 'b2')}
    del _L0_ffn_all
    return {'x': x, 'ctx_2048': ctx_2048, 'mask_BxS2_if0': mask_BxS2_if0, 'g_xattn': g_xattn, 'g_ffn': g_ffn, 'L0_xattn_W_in': _L0_xattn_in['W_in'], 'L0_xattn_b_in': _L0_xattn_in['b_in'], 'L0_xattn_g_res': _L0_xattn_in['g_res'], 'L0_xattn_g_init': _L0_xattn_in['g_init'], 'L0_ffn_norm_gamma': _L0_ffn_in['norm_gamma'], 'L0_ffn_slot_norm_gamma': _L0_ffn_in['slot_norm_gamma'], 'L0_ffn_slot_embeds': _L0_ffn_in['slot_embeds'], 'L0_ffn_w1': _L0_ffn_in['w1'], 'L0_ffn_b1': _L0_ffn_in['b1'], 'L0_ffn_w2': _L0_ffn_in['w2'], 'L0_ffn_b2': _L0_ffn_in['b2']}

def reference(x, ctx_2048, mask_BxS2_if0, g_xattn, g_ffn, L0_xattn_W_in, L0_xattn_b_in, L0_xattn_g_res, L0_xattn_g_init, L0_ffn_norm_gamma, L0_ffn_slot_norm_gamma, L0_ffn_slot_embeds, L0_ffn_w1, L0_ffn_b1, L0_ffn_w2, L0_ffn_b2):
    import jax
    import jax.numpy as jnp

    def _L0_xattn_ref(embeds, patch_embeds, patch_lens, W_in, b_in, g_res, g_init):
        import jax, jax.numpy as jnp
        import numpy as np
        B, L, P = (4, 512, 128)
        D_MODEL = 128
        D_GLOBAL = 256
        HEADDIM = 32
        EPSILON = 0.001
        RMS_EPS = 1e-05

        def rmsnorm(x, g, eps=RMS_EPS):
            var = jnp.mean(jnp.square(x), axis=-1, keepdims=True)
            return x * jax.lax.rsqrt(var + eps) * g

        def _hnet_depool(h, h_patch_full, patch_lens):
            h_patch = h_patch_full[..., :D_MODEL]
            bsz, plen = (h_patch.shape[0], h_patch.shape[1])
            seqlen = h.shape[1]
            logp = jnp.full((bsz, plen), -EPSILON, dtype=jnp.float32)
            bidx = jnp.cumsum(patch_lens, axis=1) - 1
            boundary_mask = jnp.zeros((bsz, seqlen), dtype=jnp.int32)
            boundary_mask = boundary_mask.at[jnp.arange(bsz)[:, None], bidx].set(1)
            dt = (-jnp.log(-jnp.expm1(logp))).astype(h_patch.dtype)
            x = h_patch / dt[..., None]
            n_heads = D_MODEL // HEADDIM
            A = -jnp.ones((n_heads,), dtype=jnp.float32)
            bcoef = jnp.exp(logp).astype(h_patch.dtype)
            x4 = x.reshape(bsz, plen, n_heads, HEADDIM)
            a = jnp.exp(dt[:, :, None] * A[None, None, :])
            u = (dt * bcoef)[:, :, None, None] * x4
            a_b = jnp.broadcast_to(a[..., None], u.shape)

            def comb(lft, rgt):
                aL, uL = lft
                aR, uR = rgt
                return (aL * aR, uL * aR + uR)
            _, s = jax.lax.associative_scan(comb, (a_b, u), axis=1)
            depool = s.reshape(bsz, plen, D_MODEL)
            plug = jnp.clip(jnp.cumsum(boundary_mask, axis=1) - 1, 0, plen - 1)
            depool_out = depool[jnp.arange(bsz)[:, None], plug]
            return depool_out + h
        h = rmsnorm(embeds, g_res)
        h = jnp.einsum('bld,ed->ble', h, W_in) + b_in
        h_patch = rmsnorm(patch_embeds, g_init)
        return _hnet_depool(h, h_patch, patch_lens)

    def _L0_ffn_ref(x, norm_gamma, slot_norm_gamma, slot_embeds, w1, b1, w2, b2):
        import jax, jax.numpy as jnp
        import numpy as np
        B, SEQ, DIM = (2, 512, 128)
        E, S = (8, 64)
        HID = 4 * DIM
        SCALE = DIM ** 0.5

        def rmsnorm(x, gamma):
            n = jnp.linalg.norm(x, axis=-1, keepdims=True)
            return x / jnp.maximum(n, 1e-12) * SCALE * gamma
        xn = rmsnorm(x, norm_gamma)
        sn = rmsnorm(slot_embeds, slot_norm_gamma)
        logits = jnp.einsum('bnd,esd->bnes', xn, sn)
        dispatch = jax.nn.softmax(logits, axis=1)
        b, n, e, s = logits.shape
        combine = jax.nn.softmax(logits.reshape(b, n, e * s), axis=-1)
        slots = jnp.einsum('bnd,bnes->besd', xn, dispatch)
        h = jnp.einsum('besd,edh->besh', slots, w1) + b1[None, :, None, :]
        h = jax.nn.gelu(h, approximate=False)
        eo = jnp.einsum('besh,ehd->besd', h, w2) + b2[None, :, None, :]
        eo = eo.reshape(b, e * s, DIM)
        out = jnp.einsum('bmd,bnm->bnd', eo, combine)
        return out
    x = x + jnp.tanh(g_xattn[0]) * _L0_xattn_ref(_layernorm(x, axis=-1), ctx_2048, mask_BxS2_if0, L0_xattn_W_in, L0_xattn_b_in, L0_xattn_g_res, L0_xattn_g_init)
    x = x + jnp.tanh(g_ffn[0]) * _L0_ffn_ref(_layernorm(x, axis=-1), L0_ffn_norm_gamma, L0_ffn_slot_norm_gamma, L0_ffn_slot_embeds, L0_ffn_w1, L0_ffn_b1, L0_ffn_w2, L0_ffn_b2)
    return x

_drawn_inputs = setup_inputs


def setup_inputs(seed=0):
    import zlib

    import numpy as np

    out = dict(_drawn_inputs(seed))
    spreads = {'L0_xattn_b_in': (0.0, 0.1),
     'L0_xattn_g_res': (1.0, 0.584),
     'L0_xattn_g_init': (1.0, 0.2),
     'L0_ffn_norm_gamma': (1.0, 0.2),
     'L0_ffn_slot_norm_gamma': (1.0, 0.2),
     'L0_ffn_b1': (0.0, 0.498),
     'L0_ffn_b2': (0.0, 0.1)}
    factors = {}
    for name, (base, spread) in spreads.items():
        noise = np.random.default_rng([zlib.crc32(name.encode()), seed]).standard_normal(out[name].shape)
        drawn = base * np.exp(spread * noise) if base else spread * noise
        out[name] = jnp.asarray(drawn.astype(out[name].dtype))
    for name, factor in factors.items():
        out[name] = (out[name] * factor).astype(out[name].dtype)
    return out
```

```python
from contextlib import ExitStack

import numpy as np
import concourse.bass as bass
from concourse import mybir

F32 = mybir.dt.float32
BF16 = mybir.dt.bfloat16
I32 = mybir.dt.int32
ALU = mybir.AluOpType
ACT = mybir.ActivationFunctionType
AX = mybir.AxisListType

P = 128
B, N, D = 4, 512, 128
NT = N // P
PL, DG = 77, 256
E, S = 8, 64
ES = E * S
ET = ES // P
HID = 4 * D
HT = HID // P
BS = B * S

LN_EPS = 1e-5
RMS_EPS = 1e-5
DEPOOL_EPS = 0.001
NORM_FLOOR = 1e-12

C_ID = 0
C_DEC = C_ID + P
C_TRI = C_DEC + PL + 1
C_IOTA = C_TRI + PL
C_Q = C_IOTA + N
C_BLK = C_Q + 1
C_SEL = C_BLK + B * B
C_ALL = C_SEL + B


def shape_constants():
    c = np.zeros((P, C_ALL), np.float32)
    c[:, C_ID:C_ID + P] = np.eye(P)
    dt = -np.log(-np.expm1(-DEPOOL_EPS))
    q = np.arange(PL)
    power = (q[None, :] - q[:, None]).astype(np.float64)
    decay = np.where(power >= 0, np.exp(-DEPOOL_EPS - dt * np.maximum(power, 0)), 0.0)
    c[:PL, C_DEC:C_DEC + PL] = decay
    c[PL, C_DEC + PL] = 1.0
    c[:PL, C_TRI:C_TRI + PL] = power >= 0
    c[:, C_IOTA:C_IOTA + N] = np.arange(N)
    c[:PL, C_Q] = q
    for b in range(B):
        c[:, C_BLK + b * B + b] = 1.0
        c[b, C_SEL + b] = 1.0
    return c


def flamingo_kernel(nc, x, ctx_in, lens, g_xattn, g_ffn, W_in, b_in, g_res, g_init,
                    norm_gamma, slot_gamma, slot_embeds, w1, b1, w2, b2, consts, out):
    with ExitStack() as stack:
        def sb(name, shape, dt=F32):
            return stack.enter_context(nc.sbuf_tensor(name, shape, dt))

        def ps(name, shape=(P, 512)):
            return stack.enter_context(nc.psum_tensor(name, list(shape), F32))

        def sem(name):
            return stack.enter_context(nc.semaphore(name))

        cst = sb("cst", [P, C_ALL])
        ident = cst[:, C_ID:C_ID + P]
        x_sb = sb("x_sb", [P, B, N])
        x1 = sb("x1", [P, B, N])
        y_sb = x_sb
        rows = sb("rows", [43, D])
        cols = sb("cols", [P, 43])
        gates = sb("gates", [P, 2])
        tanh_g = sb("tanh_g", [P, 2])
        gn_gs = sb("gn_gs", [P, 1])
        W_sb = sb("W_sb", [P, D])
        WT = sb("WT", [P, D])
        slot_raw = sb("slot_raw", [P, ET, D])
        slot_sq = sb("slot_sq", [P, D])
        slot_ss = sb("slot_ss", [P, ET])
        slot_n = sb("slot_n", [P, ET, D])
        snT = sb("snT", [P, ES])
        ctx_sb = sb("ctx_sb", [PL, B, DG])
        ctx_sq = sb("ctx_sq", [PL, DG])
        ctx_ss = sb("ctx_ss", [PL, B])
        ginit = sb("ginit", [PL, D])
        patch = sb("patch", [PL + 1, B, D])
        depool = sb("depool", [PL + 1, B, D])
        lens_i = sb("lens_i", [PL, B], I32)
        lens_f = sb("lens_f", [PL, B])
        bound_w = sb("bound_w", [PL, B])
        bound = sb("bound", [PL, B])
        hits = sb("hits", [PL, B, N], BF16)
        blk_bf = sb("blk_bf", [PL, B, B], BF16)
        ones_bf = sb("ones_bf", [B, PL + 1], BF16)
        mask_c = sb("mask_c", [B, N])
        cap = sb("cap", [B, N])
        count = sb("count", [B, N])
        plug = sb("plug", [B, N])
        plug_blk = sb("plug_blk", [B, B, N], BF16)
        onehot = sb("onehot", [PL + 1, N])
        half_neg = sb("half_neg", [P, NT * B])
        stats1 = sb("stats1", [P, B * NT, 6])
        mv1 = sb("mv1", [P, B * NT, 2])
        var1 = sb("var1", [P, B * NT])
        c1 = sb("c1", [P, B * NT])
        stats2 = sb("stats2", [P, NT, 6])
        mv2 = sb("mv2", [P, NT, 2])
        floor2 = sb("floor2", [P, NT])
        var2 = sb("var2", [P, NT])
        c2 = sb("c2", [P, NT])
        slot_v = sb("slot_v", [P, ET])
        slot_c = sb("slot_c", [P, ET])
        ctx_v = sb("ctx_v", [PL, B])
        ctx_c = sb("ctx_c", [PL, B])
        z1 = sb("z1", [P, NT, D])
        hT = sb("hT", [P, NT, P])
        z = sb("z", [P, NT, D])
        zs = sb("zs", [P, NT, D])
        zT = sb("zT", [P, NT, P])
        nmD = sb("nmD", [P, ET])
        nmC = sb("nmC", [P, NT])
        sumD = sb("sumD", [P, ET])
        sumC = sb("sumC", [P, NT])
        rD = sb("rD", [P, ET])
        rDb = sb("rDb", [P, ET, P])
        rC = sb("rC", [P, B, NT])
        scC = sb("scC", [P, B, NT])
        DT = sb("DT", [P, ET, N])
        Dn = sb("Dn", [P, NT, ES])
        C = sb("C", [P, NT, ES])
        CT = sb("CT", [P, B, ET, N])
        R_sb = sb("R_sb", [P, ES])
        slotsT = sb("slotsT", [P, E, B, S])
        w1_sb = sb("w1_sb", [P, E, HID])
        w2_sb = sb("w2_sb", [P, E, HT, D])
        h = sb("h", [P, 2, HT, BS])
        eoT = sb("eoT", [P, B, ES])
        eo = sb("eo", [P, ET, B, D])

        pL = [ps(f"pL{i}") for i in range(4)]
        pT = [ps(f"pT{i}") for i in range(2)]
        pM = ps("pM")
        pR = ps("pR")

        ld = {k: sem("ld_" + k) for k in ("cst", "rows", "gates", "W", "slots", "ctx", "ginit", "bin", "lens")}
        ld_x = [sem(f"ld_x{b}") for b in range(B)]
        ld_w = [sem(f"ld_w{e}") for e in range(E)]
        st_y = sem("st_y")
        s_half = sem("s_half")
        s_cap = sem("s_cap")
        s_bf = sem("s_bf")
        s_lensf = sem("s_lensf")
        s_cum = sem("s_cum")
        s_bound = sem("s_bound")
        s_hits = sem("s_hits")
        s_cnt = sem("s_cnt")
        s_plug = sem("s_plug")
        s_pb = sem("s_pb")
        s_colsp = sem("s_colsp")
        s_cols = sem("s_cols")
        s_gg = sem("s_gg")
        s_WTp = sem("s_WTp")
        s_WT = sem("s_WT")
        s_tanh = sem("s_tanh")
        s_slotss = sem("s_slotss")
        s_slotv = sem("s_slotv")
        s_slotc = sem("s_slotc")
        s_slotn = sem("s_slotn")
        s_snTp = sem("s_snTp")
        s_snT = sem("s_snT")
        s_ctxss = sem("s_ctxss")
        s_ctxv = sem("s_ctxv")
        s_ctxc = sem("s_ctxc")
        s_patch = sem("s_patch")
        s_depp = sem("s_depp")
        s_dep = sem("s_dep")
        s_dve = sem("s_dve")
        s_var1 = sem("s_var1")
        s_c1 = sem("s_c1")
        z1_ready = sem("z1_ready")
        t_done = sem("t_done")
        t_out = sem("t_out")
        bc_done = sem("bc_done")
        onehot_ready = sem("onehot_ready")
        a2_done = sem("a2_done")
        x1_ready = sem("x1_ready")
        var2_ready = sem("var2_ready")
        c2_ready = sem("c2_ready")
        z_ready = sem("z_ready")
        zs_ready = sem("zs_ready")
        logits_done = sem("logits_done")
        max_done = sem("max_done")
        expD_done = sem("expD_done")
        expC_done = sem("expC_done")
        rD_ready = sem("rD_ready")
        R_done = sem("R_done")
        R_ready = sem("R_ready")
        slots_done = sem("slots_done")
        slots_out = sem("slots_out")
        h_done = sem("h_done")
        gelu_done = sem("gelu_done")
        eoT_done = sem("eoT_done")
        eoT_ready = sem("eoT_ready")
        eo_done = sem("eo_done")
        eo_ready = sem("eo_ready")
        y_done = sem("y_done")
        y_ready = sem("y_ready")
        rC_ready = sem("rC_ready")
        sc_ready = sem("sc_ready")

        block = stack.enter_context(nc.Block())

        PER_BATCH = 2 + ET + NT

        def t_use(b, k):
            return 2 + PER_BATCH * b + k

        K_HT, K_ZT = 0, 1 + ET + NT

        def k_D(i, last):
            return i + (0 if last else 1)

        def k_C(i, last):
            return ET + i + (0 if last else 1)

        T2 = t_use(B - 1, ET + NT)

        @block.sync
        def _(sp):
            sp.dma_start(x_sb[:, 0, :], x[0].rearrange("(p t) d -> p (t d)", t=NT)).then_inc(ld_x[0], 16)
            sp.dma_start(cst[:], consts).then_inc(ld["cst"], 16)
            sp.dma_start(W_sb[:], W_in).then_inc(ld["W"], 16)
            sp.dma_start(slot_raw[:], slot_embeds.rearrange("e s d -> (e s) d").rearrange("(j p) d -> p j d", p=P)).then_inc(ld["slots"], 16)
            for b in range(1, B):
                sp.dma_start(x_sb[:, b, :], x[b].rearrange("(p t) d -> p (t d)", t=NT)).then_inc(ld_x[b], 16)
            for e in range(E):
                sp.dma_start(w1_sb[:, e, :], w1[e]).then_inc(ld_w[e], 16)
                sp.dma_start(w2_sb[:, e, :, :], w2[e].rearrange("(j p) d -> p j d", p=P)).then_inc(ld_w[e], 16)
            for b in range(B):
                sp.wait_ge(y_ready, b + 1)
                sp.dma_start(out[b].rearrange("(p t) d -> p (t d)", t=NT), y_sb[:, b, :]).then_inc(st_y, 16)
            sp.wait_ge(st_y, 16 * B)

        @block.gpsimd
        def _(pool):
            nc.gpsimd.memset(half_neg[:], -0.5).then_inc(s_half, 1)
            nc.gpsimd.memset(cap[:], float(PL)).then_inc(s_cap, 1)
            nc.gpsimd.memset(ones_bf[:, 0:PL], 1.0).then_inc(s_bf, 1)
            nc.gpsimd.memset(ones_bf[:, PL:], 0.0).then_inc(s_bf, 1)
            pool.wait_ge(ld["cst"], 16)
            nc.gpsimd.tensor_copy(blk_bf[:], cst[0:PL, C_BLK:C_BLK + B * B].rearrange("p (b c) -> p b c", b=B)).then_inc(s_bf, 1)
            pool.wait_ge(ld["lens"], 16)
            nc.gpsimd.tensor_copy(lens_f[:], lens_i[:]).then_inc(s_lensf, 1)

            def pow_half(dst, src, parts, n):
                return nc.gpsimd.tensor_tensor(dst, src, half_neg[0:parts, 0:n], ALU.pow)

            pool.wait_ge(s_half, 1)
            pool.wait_ge(s_var1, 1)
            pow_half(c1[:, 0:NT], var1[:, 0:NT], P, NT).then_inc(s_c1, 1)
            pool.wait_ge(s_ctxv, 1)
            pow_half(ctx_c[:], ctx_v[:], PL, B).then_inc(s_ctxc, 1)
            pool.wait_ge(s_slotv, 1)
            pow_half(slot_c[:], slot_v[:], P, ET).then_inc(s_slotc, 1)

            def second_scale(c):
                pool.wait_ge(var2_ready, c + 1)
                pow_half(c2[:], var2[:], P, NT).then_inc(c2_ready, 1)

            second_scale(0)
            pool.wait_ge(s_var1, 2)
            pow_half(c1[:, NT:], var1[:, NT:], P, NT * (B - 1)).then_inc(s_c1, 1)
            with pool.Fori(0, B - 1) as b:
                second_scale(b + 1)
                nc.gpsimd.tensor_copy(zs[:], z[:]).then_inc(zs_ready, 1)
            pool.wait_ge(z_ready, B)
            pool.wait_ge(slots_done, B - 1)
            nc.gpsimd.tensor_copy(zs[:], z[:]).then_inc(zs_ready, 1)

        @block.scalar
        def _(act):
            act.dma_start(lens_i[:], lens).then_inc(ld["lens"], 16)
            act.dma_start(ctx_sb[:], ctx_in.rearrange("b p d -> p b d")).then_inc(ld["ctx"], 16)
            act.dma_start(rows[0:32, :], b1.rearrange("e (j p) -> (e j) p", p=P)).then_inc(ld["rows"], 16)
            act.dma_start(rows[32:40, :], b2).then_inc(ld["rows"], 16)
            act.dma_start(rows[40:41, :], g_res.rearrange("(a d) -> a d", a=1)).then_inc(ld["rows"], 16)
            act.dma_start(rows[41:42, :], norm_gamma.rearrange("(a d) -> a d", a=1)).then_inc(ld["rows"], 16)
            act.dma_start(rows[42:43, :], slot_gamma.rearrange("(a d) -> a d", a=1)).then_inc(ld["rows"], 16)
            act.dma_start(ginit[:], g_init[0:D].rearrange("(a d) -> a d", a=1).broadcast_to([PL, D])).then_inc(ld["ginit"], 16)
            act.dma_start(patch[PL:PL + 1, :, :], b_in.rearrange("(a c d) -> a c d", a=1, c=1).broadcast_to([1, B, D])).then_inc(ld["bin"], 16)
            act.dma_start(gates[:, 0:1], g_xattn.rearrange("(a d) -> a d", a=1).broadcast_to([P, 1])).then_inc(ld["gates"], 16)
            act.dma_start(gates[:, 1:2], g_ffn.rearrange("(a d) -> a d", a=1).broadcast_to([P, 1])).then_inc(ld["gates"], 16)

            act.wait_ge(ld["ctx"], 16)
            for b in range(B):
                if b:
                    act.wait_ge(s_ctxss, b)
                nc.scalar.activation(ctx_sq[:], ctx_sb[:, b, :], ACT.Square, accum_out=ctx_ss[:, b:b + 1]).then_inc(s_ctxss, 1)
            act.wait_ge(ld["slots"], 16)
            for j in range(ET):
                if j:
                    act.wait_ge(s_slotss, j)
                nc.scalar.activation(slot_sq[:], slot_raw[:, j, :], ACT.Square, accum_out=slot_ss[:, j:j + 1]).then_inc(s_slotss, 1)
            act.wait_ge(ld["gates"], 32)
            nc.scalar.activation(tanh_g[:], gates[:], ACT.Tanh).then_inc(s_tanh, 1)

            def copy_out(u, dst, bank):
                act.wait_ge(t_done, u + 1)
                nc.scalar.activation(dst, pT[bank][:].rearrange("p (t q) -> p t q", q=P), ACT.Copy).then_inc(t_out, 1)

            def out_hT(c, u, bank):
                act.wait_ge(a2_done, c)
                copy_out(u, hT[:], bank)

            def out_zT(u, bank):
                copy_out(u, zT[:], bank)

            def exp_D(b, i):
                act.wait_ge(max_done, 8 * b + i + 1)
                nc.scalar.activation(DT[:, i, :], pL[i][:], ACT.Exp, bias=nmD[:, i:i + 1], accum_out=sumD[:, i:i + 1]).then_inc(expD_done, 1)

            def exp_C(b, i):
                act.wait_ge(max_done, 8 * b + 4 + i + 1)
                nc.scalar.activation(C[:, i, :], pL[i][:], ACT.Exp, bias=nmC[:, i:i + 1], accum_out=sumC[:, i:i + 1]).then_inc(expC_done, 1)

            def out_D(b, i, last):
                k = k_D(i, last)
                copy_out(t_use(b, k), Dn[:, :, i * P:(i + 1) * P], k % 2)

            def out_C(b, i, last):
                k = k_C(i, last)
                copy_out(t_use(b, k), CT[:, b, :, i * P:(i + 1) * P], k % 2)

            def batch(b, last):
                exp_D(b, 0)
                exp_D(b, 1)
                if not last:
                    out_hT(b + 1, t_use(b, K_HT), 0)
                exp_D(b, 2)
                exp_D(b, 3)
                exp_C(b, 0)
                exp_C(b, 1)
                out_D(b, 0, last)
                exp_C(b, 2)
                out_D(b, 1, last)
                exp_C(b, 3)
                out_D(b, 2, last)
                out_D(b, 3, last)
                out_C(b, 0, last)
                out_C(b, 1, last)
                out_C(b, 2, last)
                out_C(b, 3, last)
                if not last:
                    out_zT(t_use(b, K_ZT), 1)

            out_hT(0, 0, 0)
            out_zT(1, 1)
            with act.Fori(0, B - 1) as b:
                batch(b, False)
            batch(B - 1, True)

            act.wait_ge(s_cols, 1)
            for e in range(E):
                if e >= 2:
                    act.wait_ge(eoT_done, e - 1)
                for j in range(HT):
                    k = e * HT + j
                    act.wait_ge(h_done, k // 2 + 1)
                    nc.scalar.activation(h[:, e % 2, j, :], pL[(k // 2) % 4][:, (k % 2) * BS:(k % 2 + 1) * BS],
                                         ACT.Gelu, bias=cols[:, k:k + 1]).then_inc(gelu_done, 1)

        @block.vector
        def _(dve):
            steps = [0]

            def step(ins):
                steps[0] += 1
                ins.then_inc(s_dve, 1)
                dve.wait_ge(s_dve, steps[0])

            def mean_var1(b):
                dve.wait_ge(ld_x[b], 16)
                for t in range(NT):
                    last = nc.vector.bn_stats(stats1[:, b * NT + t, :], x_sb[:, b, t * D:(t + 1) * D])
                step(last)
                for t in range(NT):
                    last = nc.vector.bn_aggr(mv1[:, b * NT + t, :], stats1[:, b * NT + t, :])
                step(last)

            def shift_var1(b0, b1_):
                return nc.vector.tensor_scalar(var1[:, b0 * NT:b1_ * NT], mv1[:, b0 * NT:b1_ * NT, 1], 1e-10 / (1 + 1e-5), None, ALU.add)

            mean_var1(0)
            shift_var1(0, 1).then_inc(s_var1, 1)

            dve.wait_ge(s_cum, 1)
            step(nc.vector.tensor_scalar(bound_w[:], pR[0:PL, 0:B], 1.0, float(N), ALU.is_lt, ALU.mult))
            step(nc.vector.scalar_tensor_tensor(bound[:], pR[0:PL, 0:B], -1.0, bound_w[:], ALU.add, ALU.add))
            for b in range(B):
                last = nc.vector.tensor_scalar(hits[:, b, :], cst[0:PL, C_IOTA:C_IOTA + N], bound[:, b:b + 1], None, ALU.is_equal)
            last.then_inc(s_hits, 1)
            dve.wait_ge(s_c1, 1)

            def norm1(c):
                for t in range(NT):
                    last = nc.vector.tensor_scalar(z1[:, t, :], x_sb[:, c, t * D:(t + 1) * D], mv1[:, c * NT + t, 0:1],
                                                   c1[:, bass.ds(c * NT + t, 1)], ALU.subtract, ALU.mult)
                last.then_inc(z1_ready, 1)

            norm1(0)
            dve.wait_ge(s_cnt, 1)
            step(nc.vector.tensor_scalar(mask_c[:], pR[0:B, :], 1.0, None, ALU.min))
            dve.wait_ge(s_cap, 1)
            step(nc.vector.tensor_tensor_scan(count[:], mask_c[:], cap[:], 0.0, ALU.add, ALU.min))
            step(nc.vector.tensor_scalar(plug[:], count[:], -1.0, 0.0, ALU.add, ALU.max))
            for b in range(B):
                last = nc.vector.tensor_scalar(plug_blk[:, b, :], plug[:], cst[0:B, C_SEL + b:C_SEL + b + 1], None, ALU.mult)
            last.then_inc(s_plug, 1)
            dve.wait_ge(s_colsp, 1)
            nc.vector.tensor_copy(cols[:], pL[0][:, 0:43]).then_inc(s_cols, 1)
            dve.wait_ge(s_cols, 1)
            dve.wait_ge(s_WTp, 1)
            nc.vector.tensor_scalar(WT[:], pL[1][:, 0:D], cols[:, 40:41], float((1 + 1e-5) ** -0.5), ALU.mult, ALU.mult).then_inc(s_WT, 1)
            dve.wait_ge(s_ctxss, B)
            nc.vector.tensor_scalar(ctx_v[:], ctx_ss[:], 1.0 / DG, RMS_EPS, ALU.mult, ALU.add).then_inc(s_ctxv, 1)
            dve.wait_ge(s_ctxc, 1)
            dve.wait_ge(ld["ginit"], 16)
            for b in range(B):
                last = nc.vector.scalar_tensor_tensor(patch[0:PL, b, :], ctx_sb[:, b, 0:D], ctx_c[:, b:b + 1], ginit[:], ALU.mult, ALU.mult)
            last.then_inc(s_patch, 1)
            dve.wait_ge(s_slotss, ET)
            nc.vector.tensor_scalar(slot_v[:], slot_ss[:], NORM_FLOOR ** 2, 1.0 / D, ALU.max, ALU.mult).then_inc(s_slotv, 1)
            dve.wait_ge(s_depp, 1)
            nc.vector.tensor_copy(depool[:], pM[0:PL + 1, :].rearrange("p (b d) -> p b d", b=B)).then_inc(s_dep, 1)
            dve.wait_ge(s_tanh, 1)

            def make_onehot(c):
                dve.wait_ge(a2_done, c)
                dve.wait_ge(bc_done, c + 1)
                nc.vector.tensor_scalar(onehot[:], pR[0:PL + 1, :], cst[0:PL + 1, C_Q:C_Q + 1], None, ALU.is_equal).then_inc(onehot_ready, 1)

            def residual1(c):
                dve.wait_ge(a2_done, c + 1)
                nc.vector.scalar_tensor_tensor(x1[:, c, :], pM[:], tanh_g[:, 0:1], x_sb[:, c, :], ALU.mult, ALU.add).then_inc(x1_ready, 1)

            def stats_of_x1(c):
                for t in range(NT):
                    last = nc.vector.bn_stats(stats2[:, t, :], x1[:, c, t * D:(t + 1) * D])
                return last

            def aggregate():
                for t in range(NT):
                    last = nc.vector.bn_aggr(mv2[:, t, :], stats2[:, t, :])
                return last

            def clamp_var2(link):
                k = NORM_FLOOR ** 2 / D
                link(nc.vector.tensor_scalar(floor2[:], mv2[:, :, 1], LN_EPS, k, ALU.add, ALU.mult))
                nc.vector.tensor_tensor(var2[:], mv2[:, :, 1], floor2[:], ALU.max).then_inc(var2_ready, 1)

            def norm2(c):
                dve.wait_ge(c2_ready, c + 1)
                dve.wait_ge(zs_ready, c)
                for t in range(NT):
                    last = nc.vector.tensor_scalar(z[:, t, :], x1[:, c, t * D:(t + 1) * D], mv2[:, t, 0:1], c2[:, t:t + 1],
                                                   ALU.subtract, ALU.mult)
                last.then_inc(z_ready, 1)

            make_onehot(0)
            residual1(0)
            dve.wait_ge(x1_ready, 1)
            step(stats_of_x1(0))
            step(aggregate())
            clamp_var2(step)
            dve.wait_ge(s_slotc, 1)
            for j in range(ET):
                last = nc.vector.tensor_scalar(slot_n[:, j, :], slot_raw[:, j, :], slot_c[:, j:j + 1], None, ALU.mult)
            last.then_inc(s_slotn, 1)
            nc.vector.tensor_tensor(gn_gs[:], cols[:, 41:42], cols[:, 42:43], ALU.mult).then_inc(s_gg, 1)
            norm2(0)
            dve.wait_ge(s_gg, 1)
            dve.wait_ge(s_snTp, 1)
            nc.vector.tensor_scalar(snT[:], pL[2][:], gn_gs[:, 0:1], None, ALU.mult).then_inc(s_snT, 1)
            for b in range(1, B):
                mean_var1(b)
            shift_var1(1, B).then_inc(s_var1, 1)
            dve.wait_ge(s_c1, 2)

            base = steps[0]
            LINKS = 3

            def batch(b, last_b):
                links = [2]

                def link(ins):
                    links[0] += 1
                    ins.then_inc(s_dve, 1)
                    dve.wait_ge(s_dve, base + LINKS * b + links[0])

                def maxima(k, dst, i):
                    dve.wait_ge(logits_done, 8 * b + k + 1)
                    nc.vector.tensor_reduce(dst[:, i:i + 1], pL[i][:], AX.X, ALU.max, negate=True).then_inc(max_done, 1)

                if not last_b:
                    dve.wait_ge(t_done, PER_BATCH * b + 1)
                    norm1(b + 1)
                maxima(0, nmD, 0)
                maxima(1, nmD, 1)
                if not last_b:
                    make_onehot(b + 1)
                maxima(2, nmD, 2)
                maxima(3, nmD, 3)
                if not last_b:
                    residual1(b + 1)
                maxima(4, nmC, 0)
                if not last_b:
                    dve.wait_ge(x1_ready, b + 2)
                maxima(5, nmC, 1)
                if not last_b:
                    stats_of_x1(b + 1).then_inc(s_dve, 1)
                    dve.wait_ge(s_dve, base + LINKS * b + 1)
                maxima(6, nmC, 2)
                if not last_b:
                    aggregate().then_inc(s_dve, 1)
                    dve.wait_ge(s_dve, base + LINKS * b + 2)
                    clamp_var2(link)
                maxima(7, nmC, 3)
                if not last_b:
                    norm2(b + 1)
                dve.wait_ge(expD_done, 4 * b + ET)
                nc.vector.reciprocal(rD[:], sumD[:]).then_inc(rD_ready, 1)
                dve.wait_ge(expC_done, 4 * b + NT)
                nc.vector.reciprocal(rC[:, b, :], sumC[:]).then_inc(rC_ready, 1)
                dve.wait_ge(R_done, b + 1)
                nc.vector.tensor_copy(R_sb[:], pR[:]).then_inc(R_ready, 1)
                dve.wait_ge(R_ready, b + 1)
                dve.wait_ge(slots_done, b + 1)
                nc.vector.scalar_tensor_tensor(slotsT[:, :, b, :], pM[:].rearrange("p (e s) -> p e s", e=E), cols[:, 41:42],
                                               R_sb[:].rearrange("p (e s) -> p e s", e=E), ALU.mult, ALU.mult).then_inc(slots_out, 1)

            with dve.Fori(0, B - 1) as b:
                batch(b, False)
            batch(B - 1, True)

            dve.wait_ge(rC_ready, B)
            nc.vector.tensor_scalar(scC[:], rC[:], tanh_g[:, 1:2], None, ALU.mult).then_inc(sc_ready, 1)
            dve.wait_ge(sc_ready, 1)

            def out_eo(i):
                dve.wait_ge(eo_done, i + 1)
                nc.vector.tensor_copy(eo[:, i, :, :], pT[i % 2][:].rearrange("p (b d) -> p b d", b=B)).then_inc(eo_ready, 1)

            for e in range(E):
                if e >= 3 and e % 2:
                    out_eo((e - 3) // 2)
                dve.wait_ge(eoT_done, e + 1)
                bank = pM if e % 2 == 0 else pR
                nc.vector.tensor_scalar(eoT[:, :, e * S:(e + 1) * S], bank[:, 0:BS].rearrange("p (b s) -> p b s", b=B),
                                        cols[:, 32 + e:33 + e], None, ALU.add).then_inc(eoT_ready, 1)
            out_eo(ET - 1)

            for b in range(B):
                dve.wait_ge(y_done, b + 1)
                for t in range(NT):
                    last = nc.vector.scalar_tensor_tensor(y_sb[:, b, t * D:(t + 1) * D], pL[b][:, t * D:(t + 1) * D], scC[:, b, t:t + 1],
                                                          x1[:, b, t * D:(t + 1) * D], ALU.mult, ALU.add)
                last.then_inc(y_ready, 1)

        @block.tensor
        def _(pe):
            mm = nc.tensor.matmul
            pe.wait_ge(ld["cst"], 16)
            pe.wait_ge(s_lensf, 1)
            mm(pR[0:PL, 0:B], cst[0:PL, C_TRI:C_TRI + PL], lens_f[:], start=True, stop=True).then_inc(s_cum, 1)
            pe.wait_ge(ld["rows"], 80)
            nc.tensor.transpose(pL[0][:, 0:43], rows[:], cst[0:43, C_ID:C_ID + 43]).then_inc(s_colsp, 1)
            pe.wait_ge(ld["W"], 16)
            nc.tensor.transpose(pL[1][:, 0:D], W_sb[:], ident).then_inc(s_WTp, 1)

            def transposes(u, bank, srcs, free):
                if free:
                    pe.wait_ge(t_out, u - 1)
                for k, src in enumerate(srcs):
                    last = nc.tensor.transpose(pT[bank][:, k * P:(k + 1) * P], src, ident)
                last.then_inc(t_done, 1)

            def tr_hT(c, u, bank, free=True):
                pe.wait_ge(z1_ready, c + 1)
                transposes(u, bank, [z1[:, t, :] for t in range(NT)], free)

            def tr_zT(c, u, bank, free=True):
                pe.wait_ge(z_ready, c + 1)
                transposes(u, bank, [z[:, t, :] for t in range(NT)], free)

            def spread_plug(c):
                mm(pR[0:PL + 1, :], ones_bf[:], plug_blk[:, c, :].rearrange("b (p t) -> b t p", t=NT), start=True, stop=True).then_inc(bc_done, 1)

            def residual_sum(c, u):
                pe.wait_ge(t_out, u + 1)
                pe.wait_ge(onehot_ready, c + 1)
                for t in range(NT):
                    mm(pM[:, t * D:(t + 1) * D], hT[:, t, :], WT[:], start=True, stop=False)
                    last = mm(pM[:, t * D:(t + 1) * D], onehot[:, t * P:(t + 1) * P], depool[:, c, :], start=False, stop=True)
                last.then_inc(a2_done, 1)

            tr_hT(0, 0, 0, False)
            pe.wait_ge(s_bf, 3)
            pe.wait_ge(s_hits, 1)
            for b in range(B):
                last = mm(pR[0:B, :], blk_bf[:, b, :], hits[:, b, :], start=(b == 0), stop=(b == B - 1))
            last.then_inc(s_cnt, 1)
            pe.wait_ge(s_plug, 1)
            spread_plug(0)
            pe.wait_ge(ld["bin"], 16)
            pe.wait_ge(s_patch, 1)
            mm(pM[0:PL + 1, :], cst[0:PL + 1, C_DEC:C_DEC + PL + 1], patch[:].rearrange("p b d -> p (b d)"), start=True, stop=True).then_inc(s_depp, 1)
            pe.wait_ge(s_dep, 1)
            pe.wait_ge(s_WT, 1)
            residual_sum(0, 0)
            pe.wait_ge(s_slotn, 1)
            for j in range(ET):
                last = nc.tensor.transpose(pL[2][:, j * P:(j + 1) * P], slot_n[:, j, :], ident)
            last.then_inc(s_snTp, 1)
            tr_zT(0, 1, 1, False)
            pe.wait_ge(s_snT, 1)

            def batch(b, last_b):
                def logits_T(i):
                    mm(pL[i][:], snT[:, i * P:(i + 1) * P], zT[:].rearrange("d t q -> d (t q)"), start=True, stop=True).then_inc(logits_done, 1)

                def logits(i):
                    pe.wait_ge(expD_done, 4 * b + i + 1)
                    mm(pL[i][:], zT[:, i, :], snT[:], start=True, stop=True).then_inc(logits_done, 1)

                def tr_D(i):
                    k = k_D(i, last_b)
                    transposes(t_use(b, k), k % 2, [DT[:, i, t * P:(t + 1) * P] for t in range(NT)], True)

                def tr_C(i):
                    k = k_C(i, last_b)
                    pe.wait_ge(expC_done, 4 * b + i + 1)
                    transposes(t_use(b, k), k % 2, [C[:, i, j * P:(j + 1) * P] for j in range(ET)], True)

                def slots(t):
                    return mm(pM[:], zs[:, t, :], Dn[:, t, :], start=(t == 0), stop=(t == NT - 1))

                pe.wait_ge(t_out, t_use(b, 0))
                logits_T(0)
                logits_T(1)
                if not last_b:
                    tr_hT(b + 1, t_use(b, K_HT), 0)
                    spread_plug(b + 1)
                logits_T(2)
                logits_T(3)
                if not last_b:
                    residual_sum(b + 1, t_use(b, K_HT))
                logits(0)
                logits(1)
                tr_D(0)
                logits(2)
                tr_D(1)
                logits(3)
                tr_D(2)
                tr_D(3)
                pe.wait_ge(rD_ready, b + 1)
                if not last_b:
                    pe.wait_ge(onehot_ready, b + 2)
                for i in range(ET):
                    last = nc.tensor.transpose(pR[:, i * P:(i + 1) * P], rD[:, i:i + 1].broadcast_to([P, P]), ident)
                last.then_inc(R_done, 1)
                pe.wait_ge(zs_ready, b + 1)
                pe.wait_ge(t_out, t_use(b, k_D(ET - 1, last_b)) + 1)
                if not last_b:
                    pe.wait_ge(x1_ready, b + 2)
                else:
                    pe.wait_ge(slots_out, b)
                slots(0)
                tr_C(0)
                slots(1)
                tr_C(1)
                slots(2)
                tr_C(2)
                tr_C(3)
                if not last_b:
                    tr_zT(b + 1, t_use(b, K_ZT), 1)
                slots(3).then_inc(slots_done, 1)

            with pe.Fori(0, B - 1) as b:
                batch(b, False)
            batch(B - 1, True)

            def hidden(e):
                pe.wait_ge(ld_w[e], 32)
                for j in range(HT):
                    k = e * HT + j
                    if k % 2 == 0 and k >= 8:
                        pe.wait_ge(gelu_done, k - 6)
                    last = mm(pL[(k // 2) % 4][:, (k % 2) * BS:(k % 2 + 1) * BS], w1_sb[:, e, j * P:(j + 1) * P],
                              slotsT[:, e, :, :].rearrange("d b s -> d (b s)"), start=True, stop=True)
                    if k % 2:
                        last.then_inc(h_done, 1)

            def down(e):
                pe.wait_ge(gelu_done, HT * (e + 1))
                bank = pM if e % 2 == 0 else pR
                if e >= 2:
                    pe.wait_ge(eoT_ready, e - 1)
                for j in range(HT):
                    last = mm(bank[:, 0:BS], w2_sb[:, e, j, :], h[:, e % 2, j, :], start=(j == 0), stop=(j == HT - 1))
                last.then_inc(eoT_done, 1)

            def tr_eo(i):
                pe.wait_ge(eoT_ready, 2 * i + 2)
                if i >= 2:
                    pe.wait_ge(eo_ready, i - 1)
                for b in range(B):
                    last = nc.tensor.transpose(pT[i % 2][:, b * P:(b + 1) * P], eoT[:, b, i * P:(i + 1) * P], ident)
                last.then_inc(eo_done, 1)

            pe.wait_ge(slots_out, B)
            pe.wait_ge(expC_done, 4 * B)
            hidden(0)
            pe.wait_ge(t_out, T2)
            for e in range(E):
                if e + 1 < E:
                    hidden(e + 1)
                if e >= 2 and e % 2 == 0:
                    tr_eo(e // 2 - 1)
                down(e)
            tr_eo(ET - 1)
            pe.wait_ge(eo_ready, ET)
            pe.wait_ge(gelu_done, E * HT)
            for b in range(B):
                for t in range(NT):
                    for i in range(ET):
                        last = mm(pL[b][:, t * D:(t + 1) * D], CT[:, b, i, t * P:(t + 1) * P], eo[:, i, b, :], start=(i == 0), stop=(i == ET - 1))
                last.then_inc(y_done, 1)


_INS = ['x', 'ctx_2048', 'mask_BxS2_if0', 'g_xattn', 'g_ffn', 'L0_xattn_W_in', 'L0_xattn_b_in', 'L0_xattn_g_res',
        'L0_xattn_g_init', 'L0_ffn_norm_gamma', 'L0_ffn_slot_norm_gamma', 'L0_ffn_slot_embeds', 'L0_ffn_w1',
        'L0_ffn_b1', 'L0_ffn_w2', 'L0_ffn_b2']


def kernel(**inputs):
    import numpy as _np
    import concourse.bacc as _bacc
    from concourse import mybir as _mybir
    from concourse.bass_utils import run_bass_kernel_spmd as _run

    nc = _bacc.Bacc("TRN2", target_bir_lowering=False, num_devices=1)
    arrays, args = {}, []
    for name in _INS + ['shape_constants']:
        a = shape_constants() if name == 'shape_constants' else _np.asarray(inputs[name])
        if name == 'mask_BxS2_if0':
            a = a.T
        a = _np.ascontiguousarray(a)
        arrays[f"in_{name}"] = a
        args.append(nc.dram_tensor(f"in_{name}", a.shape, _mybir.dt.from_np(a.dtype), kind="ExternalInput").ap())
    y = nc.dram_tensor("out_y", (B, N, D), F32, kind="ExternalOutput").ap()
    flamingo_kernel(nc, *args, y)
    r = _run(nc, [arrays], core_ids=[0])
    return r.results[0]["out_y"]
```

```python
from contextlib import ExitStack

import numpy as np
import concourse.bass as bass
from concourse import mybir

F32 = mybir.dt.float32
BF16 = mybir.dt.bfloat16
I32 = mybir.dt.int32
ALU = mybir.AluOpType
ACT = mybir.ActivationFunctionType
AX = mybir.AxisListType

P = 128
B, N, D = 4, 512, 128
NT = N // P
PL, DG = 77, 256
E, S = 8, 64
ES = E * S
ET = ES // P
HID = 4 * D
HT = HID // P
BS = B * S

LN_EPS = 1e-5
RMS_EPS = 1e-5
DEPOOL_EPS = 0.001
NORM_FLOOR = 1e-12

VROWS = E * HT + E + 3
V_B2, V_GRES, V_NG, V_SG = E * HT, E * HT + E, E * HT + E + 1, E * HT + E + 2

C_ID = 0
C_DEC = C_ID + P
C_TRI = C_DEC + PL + 1
C_Q = C_TRI + PL
C_BLK = C_Q + 1
C_SEL = C_BLK + B * B
C_ROWS = C_SEL + B
C_GINIT = C_ROWS + D
C_GATES = C_GINIT + D
C_ALL = C_GATES + 2


def shape_constants():
    c = np.zeros((P, C_ALL), np.float32)
    c[:, C_ID:C_ID + P] = np.eye(P)
    dt = -np.log(-np.expm1(-DEPOOL_EPS))
    q = np.arange(PL)
    power = (q[None, :] - q[:, None]).astype(np.float64)
    decay = np.where(power >= 0, np.exp(-DEPOOL_EPS - dt * np.maximum(power, 0)), 0.0)
    c[:PL, C_DEC:C_DEC + PL] = decay
    c[PL, C_DEC + PL] = 1.0
    c[:PL, C_TRI:C_TRI + PL] = power >= 0
    c[:PL, C_Q] = q
    for b in range(B):
        c[:, C_BLK + b * B + b] = 1.0
        c[b, C_SEL + b] = 1.0
    return c


def flamingo_kernel(nc, x, ctx_in, lens, W_in, b_in, slot_embeds, w1, w2, small, out):
    with ExitStack() as stack:
        def sb(name, shape, dt=F32):
            return stack.enter_context(nc.sbuf_tensor(name, shape, dt))

        def ps(name, shape=(P, 512)):
            return stack.enter_context(nc.psum_tensor(name, list(shape), F32))

        def sem(name):
            return stack.enter_context(nc.semaphore(name))

        cst = sb("cst", [P, C_ALL])
        ident = cst[:, C_ID:C_ID + P]
        x_sb = sb("x_sb", [P, B, N])
        x1 = sb("x1", [P, B, N])
        y_sb = x_sb
        cols = sb("cols", [P, VROWS])
        iota = sb("iota", [PL, N])
        tanh_g = sb("tanh_g", [P, 2])
        gn_gs = sb("gn_gs", [P, 1])
        W_sb = sb("W_sb", [P, D])
        WT = sb("WT", [P, D])
        slot_raw = sb("slot_raw", [P, ET, D])
        slot_sq = sb("slot_sq", [P, D])
        slot_ss = sb("slot_ss", [P, ET])
        slot_n = sb("slot_n", [P, ET, D])
        snT = sb("snT", [P, ES])
        ctx_sb = sb("ctx_sb", [PL, B, DG])
        ctx_sq = sb("ctx_sq", [PL, DG])
        ctx_ss = sb("ctx_ss", [PL, B])
        patch = sb("patch", [PL + 1, B, D])
        depool = sb("depool", [PL + 1, B, D])
        lens_i = sb("lens_i", [PL, B], I32)
        lens_f = sb("lens_f", [PL, B])
        bound_w = sb("bound_w", [PL, B])
        bound = sb("bound", [PL, B])
        hits = sb("hits", [PL, B, N], BF16)
        blk_bf = sb("blk_bf", [PL, B, B], BF16)
        ones_bf = sb("ones_bf", [B, PL + 1], BF16)
        bound_row = sb("bound_row", [B, N])
        cap = sb("cap", [B, N])
        count = sb("count", [B, N])
        plug_blk = sb("plug_blk", [B, B, N], BF16)
        onehot = sb("onehot", [PL + 1, N])
        half_neg = sb("half_neg", [P, NT * B])
        stats1 = sb("stats1", [P, B * NT, 6])
        mv1 = sb("mv1", [P, B * NT, 2])
        var1 = sb("var1", [P, B * NT])
        c1 = sb("c1", [P, B * NT])
        stats2 = sb("stats2", [P, NT, 6])
        mv2 = sb("mv2", [P, NT, 2])
        floor2 = sb("floor2", [P, NT])
        var2 = sb("var2", [P, NT])
        c2 = sb("c2", [P, NT])
        ms = sb("ms", [P, B + ET])
        rms = sb("rms", [P, B + ET])
        z1 = sb("z1", [P, NT, D])
        hT = sb("hT", [P, NT, P])
        z = sb("z", [P, NT, D])
        zs = sb("zs", [P, NT, D])
        zT = sb("zT", [P, NT, P])
        nmD = sb("nmD", [P, ET])
        nmC = sb("nmC", [P, NT])
        sumD = sb("sumD", [P, ET])
        sumC = sb("sumC", [P, NT])
        rD = sb("rD", [P, ET])
        rDb = sb("rDb", [P, ET, P])
        rC = sb("rC", [P, B, NT])
        scC = sb("scC", [P, B, NT])
        DT = sb("DT", [P, ET, N])
        Dn = sb("Dn", [P, NT, ES])
        C = sb("C", [P, NT, ES])
        CT = sb("CT", [P, B, ET, N])
        R_sb = sb("R_sb", [P, ES])
        slotsT = sb("slotsT", [P, E, B, S])
        w1_sb = sb("w1_sb", [P, E, HID])
        w2_sb = sb("w2_sb", [P, E, HT, D])
        h = sb("h", [P, 2, HT, BS])
        eoT = sb("eoT", [P, B, ES])
        eo = sb("eo", [P, ET, B, D])

        pL = [ps(f"pL{i}") for i in range(4)]
        pT = [ps(f"pT{i}") for i in range(2)]
        pM = ps("pM")
        pR = ps("pR")

        ld = {k: sem("ld_" + k) for k in ("small", "W", "slots", "ctx", "bin", "lens")}
        ld_x = [sem(f"ld_x{b}") for b in range(B)]
        ld_w = [sem(f"ld_w{e}") for e in range(E)]
        st_y = sem("st_y")
        s_half = sem("s_half")
        s_cap = sem("s_cap")
        s_bf = sem("s_bf")
        s_lensf = sem("s_lensf")
        s_cum = sem("s_cum")
        s_bound = sem("s_bound")
        s_hits = sem("s_hits")
        s_cnt = sem("s_cnt")
        s_plug = sem("s_plug")
        s_count = sem("s_count")
        s_colsp = sem("s_colsp")
        s_cols = sem("s_cols")
        s_gg = sem("s_gg")
        s_WTp = sem("s_WTp")
        s_WT = sem("s_WT")
        s_tanh = sem("s_tanh")
        s_slotss = sem("s_slotss")
        s_slotn = sem("s_slotn")
        s_snTp = sem("s_snTp")
        s_snT = sem("s_snT")
        s_ctxss = sem("s_ctxss")
        s_iota = sem("s_iota")
        s_ms = sem("s_ms")
        s_ms0 = sem("s_ms0")
        s_msr = sem("s_msr")
        s_rms = sem("s_rms")
        s_dep0 = sem("s_dep0")
        s_patch = sem("s_patch")
        s_depp = sem("s_depp")
        s_dep = sem("s_dep")
        s_dve = sem("s_dve")
        s_var1 = sem("s_var1")
        s_c1 = sem("s_c1")
        z1_ready = sem("z1_ready")
        t_done = sem("t_done")
        t_out = sem("t_out")
        bc_done = sem("bc_done")
        onehot_ready = sem("onehot_ready")
        a2_done = sem("a2_done")
        x1_ready = sem("x1_ready")
        var2_ready = sem("var2_ready")
        c2_ready = sem("c2_ready")
        z_ready = sem("z_ready")
        zs_ready = sem("zs_ready")
        logits_done = sem("logits_done")
        max_done = sem("max_done")
        expD_done = sem("expD_done")
        expC_done = sem("expC_done")
        rD_ready = sem("rD_ready")
        R_done = sem("R_done")
        R_ready = sem("R_ready")
        slots_done = sem("slots_done")
        slots_out = sem("slots_out")
        h_done = sem("h_done")
        gelu_done = sem("gelu_done")
        eoT_done = sem("eoT_done")
        eoT_ready = sem("eoT_ready")
        eo_done = sem("eo_done")
        eo_ready = sem("eo_ready")
        y_done = sem("y_done")
        y_ready = sem("y_ready")
        rC_ready = sem("rC_ready")
        sc_ready = sem("sc_ready")

        block = stack.enter_context(nc.Block())

        PER_BATCH = 2 + ET + NT

        def t_use(b, k):
            return 2 + PER_BATCH * b + k

        K_HT, K_ZT = 0, 1 + ET + NT

        def k_D(i, last):
            return i + (0 if last else 1)

        def k_C(i, last):
            return ET + i + (0 if last else 1)

        T2 = t_use(B - 1, ET + NT)

        @block.sync
        def _(sp):
            sp.dma_start(x_sb[:, 0, :], x[0].rearrange("(p t) d -> p (t d)", t=NT)).then_inc(ld_x[0], 16)
            sp.dma_start(cst[:], small).then_inc(ld["small"], 16)
            sp.dma_start(W_sb[:], W_in).then_inc(ld["W"], 16)
            sp.dma_start(slot_raw[:], slot_embeds.rearrange("e s d -> (e s) d").rearrange("(j p) d -> p j d", p=P)).then_inc(ld["slots"], 16)
            for b in range(1, B):
                sp.dma_start(x_sb[:, b, :], x[b].rearrange("(p t) d -> p (t d)", t=NT)).then_inc(ld_x[b], 16)
            for e in range(E):
                sp.dma_start(w1_sb[:, e, :], w1[e]).then_inc(ld_w[e], 16)
                sp.dma_start(w2_sb[:, e, :, :], w2[e].rearrange("(j p) d -> p j d", p=P)).then_inc(ld_w[e], 16)
            for b in range(B):
                sp.wait_ge(y_ready, b + 1)
                sp.dma_start(out[b].rearrange("(p t) d -> p (t d)", t=NT), y_sb[:, b, :]).then_inc(st_y, 16)
            sp.wait_ge(st_y, 16 * B)

        @block.gpsimd
        def _(pool):
            nc.gpsimd.memset(half_neg[:], -0.5).then_inc(s_half, 1)
            nc.gpsimd.iota(iota[:], [[1, N]], base=0, channel_multiplier=0,
                           allow_small_or_imprecise_dtypes=True).then_inc(s_iota, 1)
            nc.gpsimd.memset(ms[:], 1.0).then_inc(s_ms, 1)
            nc.gpsimd.memset(ones_bf[:, 0:PL], 1.0).then_inc(s_bf, 1)
            nc.gpsimd.memset(ones_bf[:, PL:], 0.0).then_inc(s_bf, 1)
            pool.wait_ge(ld["lens"], 16)
            nc.gpsimd.tensor_copy(lens_f[:], lens_i[:]).then_inc(s_lensf, 1)
            pool.wait_ge(ld["small"], 16)
            nc.gpsimd.tensor_copy(blk_bf[:], cst[0:PL, C_BLK:C_BLK + B * B].rearrange("p (b c) -> p b c", b=B)).then_inc(s_bf, 1)

            def pow_half(dst, src, parts, n):
                return nc.gpsimd.tensor_tensor(dst, src, half_neg[0:parts, 0:n], ALU.pow)

            pool.wait_ge(s_half, 1)
            pool.wait_ge(s_var1, 1)
            pow_half(c1[:, 0:NT], var1[:, 0:NT], P, NT).then_inc(s_c1, 1)
            pool.wait_ge(s_ms0, 1)
            pow_half(rms[0:PL, 0:1], ms[0:PL, 0:1], PL, 1).then_inc(s_rms, 1)
            nc.gpsimd.memset(cap[:], float(PL - 1)).then_inc(s_cap, 1)
            pool.wait_ge(s_msr, 1)
            pow_half(rms[:, 1:], ms[:, 1:], P, B + ET - 1).then_inc(s_rms, 1)

            def second_scale(c):
                pool.wait_ge(var2_ready, c + 1)
                pow_half(c2[:], var2[:], P, NT).then_inc(c2_ready, 1)

            second_scale(0)
            pool.wait_ge(s_var1, 2)
            pow_half(c1[:, NT:], var1[:, NT:], P, NT * (B - 1)).then_inc(s_c1, 1)
            with pool.Fori(0, B - 1) as b:
                second_scale(b + 1)

        @block.scalar
        def _(act):
            act.dma_start(lens_i[:], lens).then_inc(ld["lens"], 16)
            act.dma_start(ctx_sb[:], ctx_in.rearrange("b p d -> p b d")).then_inc(ld["ctx"], 16)
            act.dma_start(patch[PL:PL + 1, :, :], b_in.rearrange("(a c d) -> a c d", a=1, c=1).broadcast_to([1, B, D])).then_inc(ld["bin"], 16)

            act.wait_ge(ld["ctx"], 16)
            for b in range(B):
                if b:
                    act.wait_ge(s_ctxss, b)
                nc.scalar.activation(ctx_sq[:], ctx_sb[:, b, :], ACT.Square, accum_out=ctx_ss[:, b:b + 1]).then_inc(s_ctxss, 1)
            act.wait_ge(ld["slots"], 16)
            for j in range(ET):
                if j:
                    act.wait_ge(s_slotss, j)
                nc.scalar.activation(slot_sq[:], slot_raw[:, j, :], ACT.Square, accum_out=slot_ss[:, j:j + 1]).then_inc(s_slotss, 1)
            act.wait_ge(ld["small"], 16)
            nc.scalar.activation(tanh_g[:], cst[:, C_GATES:C_GATES + 2], ACT.Tanh).then_inc(s_tanh, 1)

            def copy_out(u, dst, bank):
                act.wait_ge(t_done, u + 1)
                nc.scalar.activation(dst, pT[bank][:].rearrange("p (t q) -> p t q", q=P), ACT.Copy).then_inc(t_out, 1)

            def out_hT(c, u, bank):
                act.wait_ge(a2_done, c)
                copy_out(u, hT[:], bank)

            def out_zT(u, bank):
                copy_out(u, zT[:], bank)

            def exp_D(b, i):
                act.wait_ge(max_done, 8 * b + i + 1)
                nc.scalar.activation(DT[:, i, :], pL[i][:], ACT.Exp, bias=nmD[:, i:i + 1], accum_out=sumD[:, i:i + 1]).then_inc(expD_done, 1)

            def exp_C(b, i):
                act.wait_ge(max_done, 8 * b + 4 + i + 1)
                nc.scalar.activation(C[:, i, :], pL[i][:], ACT.Exp, bias=nmC[:, i:i + 1], accum_out=sumC[:, i:i + 1]).then_inc(expC_done, 1)

            def out_D(b, i, last):
                k = k_D(i, last)
                copy_out(t_use(b, k), Dn[:, :, i * P:(i + 1) * P], k % 2)

            def out_C(b, i, last):
                k = k_C(i, last)
                copy_out(t_use(b, k), CT[:, b, :, i * P:(i + 1) * P], k % 2)

            def batch(b, last):
                exp_D(b, 0)
                exp_D(b, 1)
                if not last:
                    out_hT(b + 1, t_use(b, K_HT), 0)
                exp_D(b, 2)
                exp_D(b, 3)
                exp_C(b, 0)
                exp_C(b, 1)
                out_D(b, 0, last)
                exp_C(b, 2)
                out_D(b, 1, last)
                exp_C(b, 3)
                out_D(b, 2, last)
                out_D(b, 3, last)
                out_C(b, 0, last)
                out_C(b, 1, last)
                out_C(b, 2, last)
                out_C(b, 3, last)
                if not last:
                    out_zT(t_use(b, K_ZT), 1)

            copy_out(0, hT[:], 0)
            act.wait_ge(s_depp, 1)
            nc.scalar.activation(depool[:, 0, :], pL[3][0:PL + 1, 0:D], ACT.Copy).then_inc(s_dep0, 1)
            act.wait_ge(s_count, 1)
            for b in range(B):
                nc.scalar.activation(plug_blk[:, b, :], count[:], ACT.Relu, scale=cst[0:B, C_SEL + b:C_SEL + b + 1]).then_inc(s_plug, 1)
            act.wait_ge(s_depp, 2)
            nc.scalar.activation(depool[:, 1:, :], pL[3][0:PL + 1, D:].rearrange("p (b d) -> p b d", d=D), ACT.Copy).then_inc(s_dep, 1)
            act.wait_ge(s_gg, 1)
            act.wait_ge(s_snTp, 1)
            nc.scalar.activation(snT[:], pL[2][:], ACT.Copy, scale=gn_gs[:, 0:1]).then_inc(s_snT, 1)
            out_zT(1, 1)
            with act.Fori(0, B - 1) as b:
                batch(b, False)
            batch(B - 1, True)

            act.wait_ge(s_cols, 1)
            for e in range(E):
                if e >= 2:
                    act.wait_ge(eoT_done, e - 1)
                for j in range(HT):
                    k = e * HT + j
                    act.wait_ge(h_done, k // 2 + 1)
                    nc.scalar.activation(h[:, e % 2, j, :], pL[(k // 2) % 4][:, (k % 2) * BS:(k % 2 + 1) * BS],
                                         ACT.Gelu, bias=cols[:, k:k + 1]).then_inc(gelu_done, 1)

        @block.vector
        def _(dve):
            steps = [0]

            def step(ins):
                steps[0] += 1
                ins.then_inc(s_dve, 1)
                dve.wait_ge(s_dve, steps[0])

            def mean_var1(b):
                dve.wait_ge(ld_x[b], 16)
                for t in range(NT):
                    last = nc.vector.bn_stats(stats1[:, b * NT + t, :], x_sb[:, b, t * D:(t + 1) * D])
                step(last)
                for t in range(NT):
                    last = nc.vector.bn_aggr(mv1[:, b * NT + t, :], stats1[:, b * NT + t, :])
                step(last)

            def shift_var1(b0, b1_):
                return nc.vector.tensor_scalar(var1[:, b0 * NT:b1_ * NT], mv1[:, b0 * NT:b1_ * NT, 1], 1e-10 / (1 + 1e-5), None, ALU.add)

            def make_onehot(c):
                dve.wait_ge(a2_done, c)
                dve.wait_ge(bc_done, c + 1)
                nc.vector.tensor_scalar(onehot[:], pR[0:PL + 1, :], cst[0:PL + 1, C_Q:C_Q + 1], None, ALU.is_equal).then_inc(onehot_ready, 1)

            def residual1(c):
                dve.wait_ge(a2_done, c + 1)
                nc.vector.scalar_tensor_tensor(x1[:, c, :], pM[:], tanh_g[:, 0:1], x_sb[:, c, :], ALU.mult, ALU.add).then_inc(x1_ready, 1)

            def stats_of_x1(c):
                for t in range(NT):
                    last = nc.vector.bn_stats(stats2[:, t, :], x1[:, c, t * D:(t + 1) * D])
                return last

            def aggregate():
                for t in range(NT):
                    last = nc.vector.bn_aggr(mv2[:, t, :], stats2[:, t, :])
                return last

            def clamp_var2(link):
                k = NORM_FLOOR ** 2 / D
                link(nc.vector.tensor_scalar(floor2[:], mv2[:, :, 1], LN_EPS, k, ALU.add, ALU.mult))
                nc.vector.tensor_tensor(var2[:], mv2[:, :, 1], floor2[:], ALU.max).then_inc(var2_ready, 1)

            def norm2(c):
                dve.wait_ge(c2_ready, c + 1)
                dve.wait_ge(zs_ready, c)
                for t in range(NT):
                    last = nc.vector.tensor_scalar(z[:, t, :], x1[:, c, t * D:(t + 1) * D], mv2[:, t, 0:1], c2[:, t:t + 1],
                                                   ALU.subtract, ALU.mult)
                last.then_inc(z_ready, 1)

            def norm1(c):
                for t in range(NT):
                    last = nc.vector.tensor_scalar(z1[:, t, :], x_sb[:, c, t * D:(t + 1) * D], mv1[:, c * NT + t, 0:1],
                                                   c1[:, bass.ds(c * NT + t, 1)], ALU.subtract, ALU.mult)
                last.then_inc(z1_ready, 1)

            def scale_patches(b0, b1_):
                for b in range(b0, b1_):
                    last = nc.vector.scalar_tensor_tensor(patch[0:PL, b, :], ctx_sb[:, b, 0:D], rms[0:PL, b:b + 1],
                                                          cst[0:PL, C_GINIT:C_GINIT + D], ALU.mult, ALU.mult)
                last.then_inc(s_patch, 1)

            mean_var1(0)
            shift_var1(0, 1).then_inc(s_var1, 1)

            dve.wait_ge(s_cum, 1)
            step(nc.vector.tensor_scalar(bound_w[:], pR[0:PL, 0:B], 1.0, float(N), ALU.is_lt, ALU.mult))
            step(nc.vector.scalar_tensor_tensor(bound[:], pR[0:PL, 0:B], -1.0, bound_w[:], ALU.add, ALU.add))
            dve.wait_ge(s_iota, 1)
            for b in range(B):
                nc.vector.tensor_scalar(hits[:, b, :], iota[:], bound[:, b:b + 1], None, ALU.is_equal).then_inc(s_hits, 1)
            dve.wait_ge(s_ms, 1)
            dve.wait_ge(s_ctxss, 1)
            nc.vector.tensor_scalar(ms[0:PL, 0:1], ctx_ss[:, 0:1], 1.0 / DG, RMS_EPS, ALU.mult, ALU.add).then_inc(s_ms0, 1)
            dve.wait_ge(s_c1, 1)
            norm1(0)
            dve.wait_ge(s_colsp, 1)
            nc.vector.tensor_copy(cols[:], pL[0][:, 0:VROWS]).then_inc(s_cols, 1)
            dve.wait_ge(s_rms, 1)
            scale_patches(0, 1)
            dve.wait_ge(s_cnt, 1)
            step(nc.vector.tensor_scalar(bound_row[:], pR[0:B, :], 1.0, None, ALU.min))
            dve.wait_ge(s_cap, 1)
            nc.vector.tensor_tensor_scan(count[:], bound_row[:], cap[:], -1.0, ALU.add, ALU.min).then_inc(s_count, 1)
            dve.wait_ge(s_cols, 1)
            dve.wait_ge(s_WTp, 1)
            nc.vector.tensor_scalar(WT[:], pL[1][:, 0:D], cols[:, V_GRES:V_GRES + 1], float((1 + 1e-5) ** -0.5), ALU.mult, ALU.mult).then_inc(s_WT, 1)
            dve.wait_ge(s_ctxss, B)
            dve.wait_ge(s_slotss, ET)
            nc.vector.tensor_scalar(ms[0:PL, 1:B], ctx_ss[:, 1:B], 1.0 / DG, RMS_EPS, ALU.mult, ALU.add)
            nc.vector.tensor_scalar(ms[:, B:], slot_ss[:], NORM_FLOOR ** 2, 1.0 / D, ALU.max, ALU.mult).then_inc(s_msr, 1)
            make_onehot(0)
            mean_var1(1)
            dve.wait_ge(s_rms, 2)
            scale_patches(1, B)
            for j in range(ET):
                last = nc.vector.tensor_scalar(slot_n[:, j, :], slot_raw[:, j, :], rms[:, B + j:B + j + 1], None, ALU.mult)
            last.then_inc(s_slotn, 1)
            nc.vector.tensor_tensor(gn_gs[:], cols[:, V_NG:V_NG + 1], cols[:, V_SG:V_SG + 1], ALU.mult).then_inc(s_gg, 1)
            dve.wait_ge(s_tanh, 1)
            residual1(0)
            dve.wait_ge(x1_ready, 1)
            step(stats_of_x1(0))
            step(aggregate())
            clamp_var2(step)
            mean_var1(2)
            norm2(0)
            mean_var1(3)
            shift_var1(1, B).then_inc(s_var1, 1)
            dve.wait_ge(s_c1, 2)

            base = steps[0]
            LINKS = 3

            def batch(b, last_b):
                links = [2]

                def link(ins):
                    links[0] += 1
                    ins.then_inc(s_dve, 1)
                    dve.wait_ge(s_dve, base + LINKS * b + links[0])

                def maxima(k, dst, i):
                    dve.wait_ge(logits_done, 8 * b + k + 1)
                    nc.vector.tensor_reduce(dst[:, i:i + 1], pL[i][:], AX.X, ALU.max, negate=True).then_inc(max_done, 1)

                if not last_b:
                    dve.wait_ge(t_done, PER_BATCH * b + 1)
                    norm1(b + 1)
                maxima(0, nmD, 0)
                dve.wait_ge(z_ready, b + 1)
                nc.vector.tensor_copy(zs[:], z[:]).then_inc(zs_ready, 1)
                maxima(1, nmD, 1)
                maxima(2, nmD, 2)
                if not last_b:
                    make_onehot(b + 1)
                maxima(3, nmD, 3)
                maxima(4, nmC, 0)
                dve.wait_ge(expD_done, 4 * b + ET)
                nc.vector.reciprocal(rD[:], sumD[:]).then_inc(rD_ready, 1)
                maxima(5, nmC, 1)
                maxima(6, nmC, 2)
                maxima(7, nmC, 3)
                if not last_b:
                    residual1(b + 1)
                    dve.wait_ge(x1_ready, b + 2)
                dve.wait_ge(expC_done, 4 * b + NT)
                nc.vector.reciprocal(rC[:, b, :], sumC[:]).then_inc(rC_ready, 1)
                if not last_b:
                    stats_of_x1(b + 1).then_inc(s_dve, 1)
                    dve.wait_ge(s_dve, base + LINKS * b + 1)
                dve.wait_ge(R_done, b + 1)
                nc.vector.tensor_copy(R_sb[:], pR[:]).then_inc(R_ready, 1)
                if not last_b:
                    aggregate().then_inc(s_dve, 1)
                    dve.wait_ge(s_dve, base + LINKS * b + 2)
                    clamp_var2(link)
                    norm2(b + 1)
                dve.wait_ge(R_ready, b + 1)
                dve.wait_ge(slots_done, b + 1)
                nc.vector.scalar_tensor_tensor(slotsT[:, :, b, :], pM[:].rearrange("p (e s) -> p e s", e=E), cols[:, V_NG:V_NG + 1],
                                               R_sb[:].rearrange("p (e s) -> p e s", e=E), ALU.mult, ALU.mult).then_inc(slots_out, 1)

            with dve.Fori(0, B - 1) as b:
                batch(b, False)
            batch(B - 1, True)

            dve.wait_ge(rC_ready, B)
            nc.vector.tensor_scalar(scC[:], rC[:], tanh_g[:, 1:2], None, ALU.mult).then_inc(sc_ready, 1)
            dve.wait_ge(sc_ready, 1)

            def out_eo(i):
                dve.wait_ge(eo_done, i + 1)
                nc.vector.tensor_copy(eo[:, i, :, :], pT[i % 2][:].rearrange("p (b d) -> p b d", b=B)).then_inc(eo_ready, 1)

            for e in range(E):
                if e >= 3 and e % 2:
                    out_eo((e - 3) // 2)
                dve.wait_ge(eoT_done, e + 1)
                bank = pM if e % 2 == 0 else pR
                nc.vector.tensor_scalar(eoT[:, :, e * S:(e + 1) * S], bank[:, 0:BS].rearrange("p (b s) -> p b s", b=B),
                                        cols[:, V_B2 + e:V_B2 + e + 1], None, ALU.add).then_inc(eoT_ready, 1)
            out_eo(ET - 1)

            for b in range(B):
                dve.wait_ge(y_done, b + 1)
                for t in range(NT):
                    last = nc.vector.scalar_tensor_tensor(y_sb[:, b, t * D:(t + 1) * D], pL[b][:, t * D:(t + 1) * D], scC[:, b, t:t + 1],
                                                          x1[:, b, t * D:(t + 1) * D], ALU.mult, ALU.add)
                last.then_inc(y_ready, 1)

        @block.tensor
        def _(pe):
            mm = nc.tensor.matmul
            pe.wait_ge(ld["small"], 16)
            pe.wait_ge(s_lensf, 1)
            mm(pR[0:PL, 0:B], cst[0:PL, C_TRI:C_TRI + PL], lens_f[:], start=True, stop=True).then_inc(s_cum, 1)
            nc.tensor.transpose(pL[0][:, 0:VROWS], cst[0:VROWS, C_ROWS:C_ROWS + D], cst[0:VROWS, C_ID:C_ID + VROWS]).then_inc(s_colsp, 1)
            pe.wait_ge(ld["W"], 16)
            nc.tensor.transpose(pL[1][:, 0:D], W_sb[:], ident).then_inc(s_WTp, 1)

            def transposes(u, bank, srcs, free):
                if free:
                    pe.wait_ge(t_out, u - 1)
                for k, src in enumerate(srcs):
                    last = nc.tensor.transpose(pT[bank][:, k * P:(k + 1) * P], src, ident)
                last.then_inc(t_done, 1)

            def tr_hT(c, u, bank, free=True):
                pe.wait_ge(z1_ready, c + 1)
                transposes(u, bank, [z1[:, t, :] for t in range(NT)], free)

            def tr_zT(c, u, bank, free=True):
                pe.wait_ge(z_ready, c + 1)
                transposes(u, bank, [z[:, t, :] for t in range(NT)], free)

            def spread_plug(c):
                mm(pR[0:PL + 1, :], ones_bf[:], plug_blk[:, c, :].rearrange("b (p t) -> b t p", t=NT), start=True, stop=True).then_inc(bc_done, 1)

            def residual_sum(c, u):
                pe.wait_ge(t_out, u + 1)
                pe.wait_ge(onehot_ready, c + 1)
                for t in range(NT):
                    mm(pM[:, t * D:(t + 1) * D], hT[:, t, :], WT[:], start=True, stop=False)
                    last = mm(pM[:, t * D:(t + 1) * D], onehot[:, t * P:(t + 1) * P], depool[:, c, :], start=False, stop=True)
                last.then_inc(a2_done, 1)

            pe.wait_ge(s_bf, 3)
            for b in range(B):
                pe.wait_ge(s_hits, b + 1)
                last = mm(pR[0:B, :], blk_bf[:, b, :], hits[:, b, :], start=(b == 0), stop=(b == B - 1))
            last.then_inc(s_cnt, 1)
            tr_hT(0, 0, 0, False)
            pe.wait_ge(ld["bin"], 16)
            pe.wait_ge(s_patch, 1)
            mm(pL[3][0:PL + 1, 0:D], cst[0:PL + 1, C_DEC:C_DEC + PL + 1], patch[:, 0, :], start=True, stop=True).then_inc(s_depp, 1)
            pe.wait_ge(s_plug, 1)
            spread_plug(0)
            pe.wait_ge(s_dep0, 1)
            pe.wait_ge(s_WT, 1)
            residual_sum(0, 0)
            pe.wait_ge(s_patch, 2)
            mm(pL[3][0:PL + 1, D:], cst[0:PL + 1, C_DEC:C_DEC + PL + 1], patch[:, 1:, :].rearrange("p b d -> p (b d)"), start=True, stop=True).then_inc(s_depp, 1)
            pe.wait_ge(s_slotn, 1)
            for j in range(ET):
                last = nc.tensor.transpose(pL[2][:, j * P:(j + 1) * P], slot_n[:, j, :], ident)
            last.then_inc(s_snTp, 1)
            tr_zT(0, 1, 1, False)
            pe.wait_ge(s_snT, 1)
            pe.wait_ge(s_dep, 1)
            pe.wait_ge(s_plug, B)

            def batch(b, last_b):
                def logits_T(i):
                    mm(pL[i][:], snT[:, i * P:(i + 1) * P], zT[:].rearrange("d t q -> d (t q)"), start=True, stop=True).then_inc(logits_done, 1)

                def logits(i):
                    pe.wait_ge(expD_done, 4 * b + i + 1)
                    mm(pL[i][:], zT[:, i, :], snT[:], start=True, stop=True).then_inc(logits_done, 1)

                def tr_D(i):
                    k = k_D(i, last_b)
                    transposes(t_use(b, k), k % 2, [DT[:, i, t * P:(t + 1) * P] for t in range(NT)], True)

                def tr_C(i):
                    k = k_C(i, last_b)
                    pe.wait_ge(expC_done, 4 * b + i + 1)
                    transposes(t_use(b, k), k % 2, [C[:, i, j * P:(j + 1) * P] for j in range(ET)], True)

                def slots(t):
                    return mm(pM[:], zs[:, t, :], Dn[:, t, :], start=(t == 0), stop=(t == NT - 1))

                pe.wait_ge(t_out, t_use(b, 0))
                logits_T(0)
                logits_T(1)
                logits_T(2)
                if not last_b:
                    tr_hT(b + 1, t_use(b, K_HT), 0)
                    spread_plug(b + 1)
                logits_T(3)
                logits(0)
                logits(1)
                tr_D(0)
                logits(2)
                tr_D(1)
                logits(3)
                if not last_b:
                    residual_sum(b + 1, t_use(b, K_HT))
                tr_D(2)
                tr_D(3)
                pe.wait_ge(rD_ready, b + 1)
                if not last_b:
                    pe.wait_ge(onehot_ready, b + 2)
                for i in range(ET):
                    last = nc.tensor.transpose(pR[:, i * P:(i + 1) * P], rD[:, i:i + 1].broadcast_to([P, P]), ident)
                last.then_inc(R_done, 1)
                tr_C(0)
                pe.wait_ge(zs_ready, b + 1)
                pe.wait_ge(t_out, t_use(b, k_D(ET - 1, last_b)) + 1)
                if not last_b:
                    pe.wait_ge(x1_ready, b + 2)
                else:
                    pe.wait_ge(slots_out, b)
                slots(0)
                tr_C(1)
                slots(1)
                if not last_b:
                    tr_C(2)
                    slots(2)
                    tr_C(3)
                    tr_zT(b + 1, t_use(b, K_ZT), 1)
                    slots(3).then_inc(slots_done, 1)
                else:
                    slots(2)
                    slots(3).then_inc(slots_done, 1)
                    tr_C(2)
                    tr_C(3)

            with pe.Fori(0, B - 1) as b:
                batch(b, False)
            batch(B - 1, True)

            def hidden(e):
                pe.wait_ge(ld_w[e], 32)
                for j in range(HT):
                    k = e * HT + j
                    if k % 2 == 0 and k >= 8:
                        pe.wait_ge(gelu_done, k - 6)
                    last = mm(pL[(k // 2) % 4][:, (k % 2) * BS:(k % 2 + 1) * BS], w1_sb[:, e, j * P:(j + 1) * P],
                              slotsT[:, e, :, :].rearrange("d b s -> d (b s)"), start=True, stop=True)
                    if k % 2:
                        last.then_inc(h_done, 1)

            def down(e):
                pe.wait_ge(gelu_done, HT * (e + 1))
                bank = pM if e % 2 == 0 else pR
                if e >= 2:
                    pe.wait_ge(eoT_ready, e - 1)
                for j in range(HT):
                    last = mm(bank[:, 0:BS], w2_sb[:, e, j, :], h[:, e % 2, j, :], start=(j == 0), stop=(j == HT - 1))
                last.then_inc(eoT_done, 1)

            def tr_eo(i):
                pe.wait_ge(eoT_ready, 2 * i + 2)
                if i >= 2:
                    pe.wait_ge(eo_ready, i - 1)
                for b in range(B):
                    last = nc.tensor.transpose(pT[i % 2][:, b * P:(b + 1) * P], eoT[:, b, i * P:(i + 1) * P], ident)
                last.then_inc(eo_done, 1)

            pe.wait_ge(slots_out, B)
            pe.wait_ge(expC_done, 4 * B)
            hidden(0)
            pe.wait_ge(t_out, T2)
            for e in range(E):
                if e + 1 < E:
                    hidden(e + 1)
                if e >= 2 and e % 2 == 0:
                    tr_eo(e // 2 - 1)
                down(e)
            tr_eo(ET - 1)
            pe.wait_ge(eo_ready, ET)
            pe.wait_ge(gelu_done, E * HT)
            for b in range(B):
                for t in range(NT):
                    for i in range(ET):
                        last = mm(pL[b][:, t * D:(t + 1) * D], CT[:, b, i, t * P:(t + 1) * P], eo[:, i, b, :], start=(i == 0), stop=(i == ET - 1))
                last.then_inc(y_done, 1)


_INS = ['x', 'ctx_2048', 'mask_BxS2_if0', 'L0_xattn_W_in', 'L0_xattn_b_in', 'L0_ffn_slot_embeds', 'L0_ffn_w1',
        'L0_ffn_w2', 'small']


def kernel(**inputs):
    import numpy as _np
    import concourse.bacc as _bacc
    from concourse import mybir as _mybir
    from concourse.bass_utils import run_bass_kernel_spmd as _run

    given = {k: _np.asarray(v) for k, v in inputs.items()}
    given['mask_BxS2_if0'] = given['mask_BxS2_if0'].T
    small = shape_constants()
    rows = [given['L0_ffn_b1'].reshape(E * HT, D), given['L0_ffn_b2'], given['L0_xattn_g_res'].reshape(1, D),
            given['L0_ffn_norm_gamma'].reshape(1, D), given['L0_ffn_slot_norm_gamma'].reshape(1, D)]
    small[:VROWS, C_ROWS:C_ROWS + D] = _np.concatenate(rows)
    small[:, C_GINIT:C_GINIT + D] = given['L0_xattn_g_init'][:D]
    small[:, C_GATES] = given['g_xattn']
    small[:, C_GATES + 1] = given['g_ffn']
    given['small'] = small

    nc = _bacc.Bacc("TRN2", target_bir_lowering=False, num_devices=1)
    arrays, args = {}, []
    for name in _INS:
        a = _np.ascontiguousarray(given[name])
        arrays[f"in_{name}"] = a
        args.append(nc.dram_tensor(f"in_{name}", a.shape, _mybir.dt.from_np(a.dtype), kind="ExternalInput").ap())
    y = nc.dram_tensor("out_y", (B, N, D), F32, kind="ExternalOutput").ap()
    flamingo_kernel(nc, *args, y)
    r = _run(nc, [arrays], core_ids=[0])
    return r.results[0]["out_y"]
```

```python
from contextlib import ExitStack

import numpy as np
import concourse.bass as bass
from concourse import mybir

F32 = mybir.dt.float32
BF16 = mybir.dt.bfloat16
F32R = mybir.dt.float32r
I32 = mybir.dt.int32
ALU = mybir.AluOpType
ACT = mybir.ActivationFunctionType
AX = mybir.AxisListType

P = 128
B, N, D = 4, 512, 128
NT = N // P
PL, DG = 77, 256
E, S = 8, 64
ES = E * S
ET = ES // P
HID = 4 * D
HT = HID // P
BS = B * S

LN_EPS = 1e-5
RMS_EPS = 1e-5
DEPOOL_EPS = 0.001
NORM_FLOOR = 1e-12
NORM1_GAIN = float((1 + RMS_EPS) ** -0.5)
NORM1_SHIFT = LN_EPS * RMS_EPS / (1 + RMS_EPS)

VROWS = E * HT + E + 3
V_B2, V_GRES, V_NG, V_SG = E * HT, E * HT + E, E * HT + E + 1, E * HT + E + 2

C_ID = 0
C_DEC = C_ID + P
C_TRI = C_DEC + PL + 1
C_Q = C_TRI + PL
C_BLK = C_Q + 1
C_SEL = C_BLK + B * B
C_ROWS = C_SEL + B
C_GINIT = C_ROWS + D
C_GATES = C_GINIT + D
C_ALL = C_GATES + 2


def shape_constants():
    c = np.zeros((P, C_ALL), np.float32)
    c[:, C_ID:C_ID + P] = np.eye(P)
    dt = -np.log(-np.expm1(-DEPOOL_EPS))
    q = np.arange(PL)
    power = (q[None, :] - q[:, None]).astype(np.float64)
    decay = np.where(power >= 0, np.exp(-DEPOOL_EPS - dt * np.maximum(power, 0)), 0.0)
    c[:PL, C_DEC:C_DEC + PL] = decay
    c[PL, C_DEC + PL] = 1.0
    c[:PL, C_TRI:C_TRI + PL] = power >= 0
    c[:PL, C_Q] = q
    for b in range(B):
        c[:, C_BLK + b * B + b] = 1.0
        c[b, C_SEL + b] = 1.0
    return c


def flamingo_kernel(nc, x, ctx_in, lens, W_in, b_in, slot_embeds, w1, w2, small, out):
    with ExitStack() as stack:
        def sb(name, shape, dt=F32):
            return stack.enter_context(nc.sbuf_tensor(name, shape, dt))

        def ps(name, shape=(P, 512)):
            return stack.enter_context(nc.psum_tensor(name, list(shape), F32))

        def sem(name):
            return stack.enter_context(nc.semaphore(name))

        cst = sb("cst", [P, C_ALL])
        ident = cst[:, C_ID:C_ID + P]
        x_sb = sb("x_sb", [P, B, N])
        x1 = sb("x1", [P, B, N])
        y_sb = x_sb
        cols = sb("cols", [P, VROWS])
        tanh_g = sb("tanh_g", [P, 2])
        gn_gs = sb("gn_gs", [P, 1])
        W_sb = sb("W_sb", [P, D])
        WT = sb("WT", [P, D])
        slot_sq = sb("slot_sq", [P, D])
        slot_ss = sb("slot_ss", [P, ET])
        snT = sb("snT", [P, ES])
        snT_hi = sb("snT_hi", [P, ES], F32R)
        snT_lo = sb("snT_lo", [P, ES], F32R)
        ctx_sq = sb("ctx_sq", [PL, DG])
        ctx_ss = sb("ctx_ss", [PL, B])
        patch = sb("patch", [PL + 1, B, D])
        depool = sb("depool", [PL + 1, B, D])
        lens_i = sb("lens_i", [PL, B], I32)
        lens_f = sb("lens_f", [PL, B])
        bound_w = sb("bound_w", [PL, B])
        bound = sb("bound", [PL, B])
        blk_bf = sb("blk_bf", [PL, B, B], BF16)
        ones_bf = sb("ones_bf", [B, PL + 1], BF16)
        onehot = sb("onehot", [PL + 1, N])
        warm = sb("warm", [P, N], BF16)
        half_neg = sb("half_neg", [P, NT * B])
        gelu_try = sb("gelu_try", [P, 1])
        stats1 = sb("stats1", [P, B * NT, 6])
        mv1 = sb("mv1", [P, B * NT, 2])
        var1 = sb("var1", [P, B * NT])
        c1 = sb("c1", [P, B * NT])
        stats2 = sb("stats2", [P, NT, 6])
        mv2 = sb("mv2", [P, NT, 2])
        floor2 = sb("floor2", [P, NT])
        var2 = sb("var2", [P, NT])
        c2 = sb("c2", [P, NT])
        ms = sb("ms", [P, B + ET])
        rms = sb("rms", [P, B + ET])
        z1 = sb("z1", [P, NT, D])
        hT = sb("hT", [P, NT, P])
        z = sb("z", [P, NT, D])
        zs = sb("zs", [P, B, NT, D + 1])
        zT_hi = sb("zT_hi", [P, NT, P], F32R)
        zT_lo = sb("zT_lo", [P, NT, P], F32R)
        logits0 = sb("logits0", [P, ES])
        cmax = sb("cmax", [P, ES])
        nmD = sb("nmD", [P, ET])
        nm_rows = sb("nm_rows", [P, ES])
        nmC = sb("nmC", [P, NT])
        sumC = sb("sumC", [P, NT])
        rD = sb("rD", [P, ET])
        rC = sb("rC", [P, B, NT])
        scC = sb("scC", [P, B, NT])
        Dn = sb("Dn", [P, NT, ES])
        C = sb("C", [P, NT, ES])
        CT = sb("CT", [P, B, ET, N])
        iota = CT[0:PL, B - 1, 0, :]
        bound_row = CT[0:B, B - 1, 1, :]
        cap = CT[0:B, B - 1, 2, :]
        count = CT[0:B, B - 1, 3, :]
        slots_sb = sb("slots_sb", [P, ET, D])
        slotsT = sb("slotsT", [P, E, S])
        slotsT_hi = sb("slotsT_hi", [P, E, B, S], F32R)
        slotsT_lo = sb("slotsT_lo", [P, E, B, S], F32R)
        w1_sb = sb("w1_sb", [P, E, HID])
        w1_hi = sb("w1_hi", [P, E, HID], F32R)
        w1_lo = sb("w1_lo", [P, E, HID], F32R)
        w2_sb = sb("w2_sb", [P, E, HT, D])
        h = C[:].rearrange("p t q -> p (t q)").rearrange("p (u j q) -> p u j q", u=2, j=HT)
        Dn_flat = Dn[:].rearrange("p t q -> p (t q)")
        slot_raw = Dn_flat[:, 0:ET * D].rearrange("p (j d) -> p j d", d=D)
        slot_n = Dn_flat[:, ET * D:2 * ET * D].rearrange("p (j d) -> p j d", d=D)
        hits = Dn_flat[0:PL, 2 * ET * D:2 * ET * D + B * N // 2].bitcast(BF16).rearrange("p (b n) -> p b n", b=B)
        eoT = zs[:].rearrange("p b t d -> p (b t d)")[:, 0:B * ES].rearrange("p (b q) -> p b q", b=B)
        eo = sb("eo", [P, ET, B, D])
        eo_flat = eo[:].rearrange("p j b d -> p (j b d)")
        ctx_sb = eo_flat[0:PL, 0:B * DG].rearrange("p (b d) -> p b d", b=B)
        plug_blk = eo_flat[0:B, B * DG:B * DG + B * N // 2].bitcast(BF16).rearrange("p (b n) -> p b n", b=B)

        pL = [ps(f"pL{i}") for i in range(4)]
        pT = [ps(f"pT{i}") for i in range(2)]
        pM = ps("pM")
        pR = ps("pR")

        last_banks = [pL[3], pM, pR, pT[0]]

        ld = {k: sem("ld_" + k) for k in ("small", "W", "slots", "ctx", "bin", "lens")}
        ld_x = [sem(f"ld_x{b}") for b in range(B)]
        ld_w = sem("ld_w")
        w_hi_ready = sem("w_hi_ready")
        w_lo_ready = sem("w_lo_ready")
        slotsT_hi_ready = sem("slotsT_hi_ready")
        slotsT_split = sem("slotsT_split")
        slotsT_lo_last = sem("slotsT_lo_last")
        st_y = sem("st_y")
        s_warm = sem("s_warm")
        s_half = sem("s_half")
        s_cap = sem("s_cap")
        s_bf = sem("s_bf")
        s_lensf = sem("s_lensf")
        s_cum = sem("s_cum")
        s_hits = sem("s_hits")
        s_cnt = sem("s_cnt")
        s_plug = sem("s_plug")
        s_count = sem("s_count")
        s_colsp = sem("s_colsp")
        s_cols = sem("s_cols")
        s_gg = sem("s_gg")
        s_WTp = sem("s_WTp")
        s_WT = sem("s_WT")
        s_tanh = sem("s_tanh")
        s_slotss = sem("s_slotss")
        s_slotn = sem("s_slotn")
        s_snTp = sem("s_snTp")
        s_snT = sem("s_snT")
        s_ctxss = sem("s_ctxss")
        s_iota = sem("s_iota")
        s_ms = sem("s_ms")
        s_ms0 = sem("s_ms0")
        s_msr = sem("s_msr")
        s_rms = sem("s_rms")
        s_dep0 = sem("s_dep0")
        s_patch = sem("s_patch")
        s_depp = sem("s_depp")
        s_dep = sem("s_dep")
        s_dve = sem("s_dve")
        s_var1 = sem("s_var1")
        s_c1 = sem("s_c1")
        s_centred = sem("s_centred")
        s_centred2 = sem("s_centred2")
        shifted0 = sem("shifted0")
        z1_ready = sem("z1_ready")
        t_done = sem("t_done")
        t_out = sem("t_out")
        bc_done = sem("bc_done")
        onehot_ready = sem("onehot_ready")
        a2_done = sem("a2_done")
        x1_ready = sem("x1_ready")
        var2_ready = sem("var2_ready")
        c2_ready = sem("c2_ready")
        z_ready = sem("z_ready")
        zlo_ready = sem("zlo_ready")
        snlo_ready = sem("snlo_ready")
        zp_ready = sem("zp_ready")
        zs_ready = sem("zs_ready")
        stats2_ready = sem("stats2_ready")
        mv2_ready = sem("mv2_ready")
        logits_done = sem("logits_done")
        max_done = sem("max_done")
        expD_done = sem("expD_done")
        expC_done = sem("expC_done")
        logits0_kept = sem("logits0_kept")
        cmaxT_done = sem("cmaxT_done")
        nm_ready = sem("nm_ready")
        nmT_done = sem("nmT_done")
        nm_rows_ready = sem("nm_rows_ready")
        shifted = sem("shifted")
        slotsT_done = sem("slotsT_done")
        slotsT_ready = sem("slotsT_ready")
        s_ones = sem("s_ones")
        slots_done = sem("slots_done")
        slots_out = sem("slots_out")
        h_done = sem("h_done")
        gelu_done = sem("gelu_done")
        eoT_done = sem("eoT_done")
        eoT_ready = sem("eoT_ready")
        eo_done = sem("eo_done")
        eo_ready = sem("eo_ready")
        y_done = sem("y_done")
        y_ready = sem("y_ready")
        y_tile_done = sem("y_tile_done")
        y_tile_ready = sem("y_tile_ready")
        rC_ready = sem("rC_ready")
        sc_ready = sem("sc_ready")

        block = stack.enter_context(nc.Block())

        PER_TURN = NT + 2
        FIRST = 3 + NT
        HALF = NT // 2
        FE = P // S

        def t_hT(c):
            return FIRST + PER_TURN * (c - 2), 1

        def t_zT(c):
            return FIRST + PER_TURN * (c - 2) + 4, 1

        def t_C(b, i, ahead):
            if i == NT - 1:
                if ahead > 1:
                    return FIRST + PER_TURN * b + 1, 0
                u = FIRST + PER_TURN * (B - 2) + (0 if ahead else NT)
            else:
                if ahead:
                    return FIRST + PER_TURN * (b - 1) + (2, 3, 5)[i], (1, 0, 0)[i]
                u = FIRST + PER_TURN * (b - 1) + 1 + i
            return u, u % 2

        EARLIER_USES = t_C(B - 1, NT - 1, 0)[0] + 1

        @block.sync
        def _(sp):
            sp.dma_start(x_sb[:, 0, :], x[0].rearrange("(p t) d -> p (t d)", t=NT)).then_inc(ld_x[0], 16)
            sp.dma_start(cst[:], small).then_inc(ld["small"], 16)
            sp.dma_start(W_sb[:], W_in).then_inc(ld["W"], 16)
            sp.dma_start(slot_raw, slot_embeds.rearrange("e s d -> (e s) d").rearrange("(j p) d -> p j d", p=P)).then_inc(ld["slots"], 16)
            for b in range(1, B):
                sp.dma_start(x_sb[:, b, :], x[b].rearrange("(p t) d -> p (t d)", t=NT)).then_inc(ld_x[b], 16)
            for e in range(E):
                sp.dma_start(w1_sb[:, e, :], w1[e]).then_inc(ld_w, 16)
                sp.dma_start(w2_sb[:, e, :, :], w2[e].rearrange("(j p) d -> p j d", p=P)).then_inc(ld_w, 16)
            for b in range(B - 1):
                sp.wait_ge(y_ready, b + 1)
                sp.dma_start(out[b].rearrange("(p t) d -> p (t d)", t=NT), y_sb[:, b, :]).then_inc(st_y, 16)
            for k in range(2):
                sp.wait_ge(y_tile_ready, (k + 1) * HALF)
                sp.dma_start(out[B - 1].rearrange("(p t) d -> p (t d)", t=NT)[:, k * HALF * D:(k + 1) * HALF * D],
                             y_sb[:, B - 1, k * HALF * D:(k + 1) * HALF * D]).then_inc(st_y, 16)
            sp.wait_ge(st_y, 16 * (B + 1))

        @block.gpsimd
        def _(pool):
            nc.gpsimd.memset(half_neg[:], -0.5).then_inc(s_half, 1)
            nc.gpsimd.iota(iota, [[1, N]], base=0, channel_multiplier=0,
                           allow_small_or_imprecise_dtypes=True).then_inc(s_iota, 1)
            nc.gpsimd.memset(ms[:], 1.0).then_inc(s_ms, 1)
            nc.gpsimd.memset(ones_bf[:, 0:PL], 1.0).then_inc(s_bf, 1)
            nc.gpsimd.memset(ones_bf[:, PL:], 0.0).then_inc(s_bf, 1)
            pool.wait_ge(ld["lens"], 16)
            nc.gpsimd.tensor_copy(lens_f[:], lens_i[:]).then_inc(s_lensf, 1)
            pool.wait_ge(ld["small"], 16)
            nc.gpsimd.tensor_copy(blk_bf[:], cst[0:PL, C_BLK:C_BLK + B * B].rearrange("p (b c) -> p b c", b=B)).then_inc(s_bf, 1)

            nc.gpsimd.memset(zs[:, :, :, D:], 1.0).then_inc(s_ones, 1)

            def pow_half(dst, src, parts, n):
                return nc.gpsimd.tensor_tensor(dst, src, half_neg[0:parts, 0:n], ALU.pow)

            pool.wait_ge(s_half, 1)
            pool.wait_ge(s_var1, 1)
            pow_half(c1[:, 0:NT], var1[:, 0:NT], P, NT).then_inc(s_c1, 1)
            pool.wait_ge(s_ms0, 1)
            pow_half(rms[0:PL, 0:1], ms[0:PL, 0:1], PL, 1).then_inc(s_rms, 1)
            nc.gpsimd.memset(cap, float(PL - 1)).then_inc(s_cap, 1)
            pool.wait_ge(s_msr, 1)
            pow_half(rms[:, 1:], ms[:, 1:], P, B + ET - 1).then_inc(s_rms, 1)
            pool.wait_ge(s_var1, 2)
            pow_half(c1[:, NT:2 * NT], var1[:, NT:2 * NT], P, NT).then_inc(s_c1, 1)

            def second_scale(c):
                pool.wait_ge(var2_ready, c + 1)
                pow_half(c2[:], var2[:], P, NT).then_inc(c2_ready, 1)

            def norm1(c):
                tiles = bass.ds(c * NT, NT)
                mean = mv1[:, tiles, 0:1].broadcast_to([P, NT, D])
                nc.gpsimd.tensor_tensor(z1[:], x_sb[:, c, :].rearrange("p (t d) -> p t d", d=D), mean, ALU.subtract).then_inc(s_centred, 1)
                pool.wait_ge(s_centred, c)
                nc.gpsimd.tensor_tensor(z1[:], z1[:], c1[:, tiles].rearrange("p (t a) -> p t a", a=1).broadcast_to([P, NT, D]), ALU.mult).then_inc(z1_ready, 1)

            def keep_z(c):
                pool.wait_ge(z_ready, c + 1)
                if not isinstance(c, int) or c:
                    pool.wait_ge(zp_ready, c)
                nc.gpsimd.tensor_tensor(zs[:, c, :, 0:D], z[:], zs[:, 0, :, D:].broadcast_to([P, NT, D]), ALU.mult).then_inc(zs_ready, 1)

            def norm2(c):
                pool.wait_ge(zlo_ready, c)
                pool.wait_ge(zs_ready, c)
                pool.wait_ge(mv2_ready, c + 1)
                nc.gpsimd.tensor_tensor(z[:, HALF:, :], x1[:, c, HALF * D:].rearrange("p (t d) -> p t d", d=D),
                                        mv2[:, HALF:, 0:1].broadcast_to([P, NT - HALF, D]), ALU.subtract).then_inc(s_centred2, 1)
                second_scale(c)
                pool.wait_ge(c2_ready, c + 1)
                pool.wait_ge(s_centred2, c)
                nc.gpsimd.tensor_tensor(z[:, HALF:, :], z[:, HALF:, :], c2[:, HALF:].rearrange("p (t a) -> p t a", a=1).broadcast_to([P, NT - HALF, D]),
                                        ALU.mult).then_inc(zp_ready, 1)

            def shift0(b):
                pool.wait_ge(nm_rows_ready, b + 1)
                nc.gpsimd.tensor_tensor(Dn[:, 0, :], logits0[:], nm_rows[:], ALU.add).then_inc(shifted0, 1)

            pool.wait_ge(s_c1, 2)
            norm1(1)
            second_scale(0)
            keep_z(0)
            norm2(1)
            keep_z(1)
            pool.wait_ge(s_var1, 3)
            pow_half(c1[:, 2 * NT:3 * NT], var1[:, 2 * NT:3 * NT], P, NT).then_inc(s_c1, 1)
            pool.wait_ge(s_c1, 3)
            pool.wait_ge(t_done, 2)
            norm1(2)

            def split_w1(b):
                for k in range(2):
                    pool.wait_ge(w_hi_ready, 2 * b + k + 1)
                    nc.gpsimd.tensor_tensor(w1_lo[:, 2 * b + k, :], w1_sb[:, 2 * b + k, :], w1_hi[:, 2 * b + k, :].bitcast(F32),
                                            ALU.subtract).then_inc(w_lo_ready, 1)

            def split_slotsT(b):
                pool.wait_ge(slotsT_ready, b + 1)
                nc.gpsimd.tensor_tensor(slotsT_lo[:, :, b, :], slotsT[:], slotsT_hi[:, :, b, :].bitcast(F32), ALU.subtract).then_inc(slotsT_split, 1)

            def turn(b, more):
                split_w1(b)
                norm2(b + 2)
                keep_z(b + 2)
                if more:
                    norm1(b + 3)
                shift0(b + 1)
                split_slotsT(b)

            shift0(0)
            pool.wait_ge(s_var1, 4)
            pow_half(c1[:, 3 * NT:], var1[:, 3 * NT:], P, NT * (B - 3)).then_inc(s_c1, 1)
            pool.wait_ge(s_c1, 4)
            with pool.Fori(0, B - 3) as b:
                turn(b, True)
            turn(B - 3, False)
            split_w1(B - 2)
            split_slotsT(B - 2)
            split_w1(B - 1)

        @block.scalar
        def _(act):
            act.dma_start(lens_i[:], lens).then_inc(ld["lens"], 16)
            act.dma_start(ctx_sb, ctx_in.rearrange("b p d -> p b d")).then_inc(ld["ctx"], 16)
            act.dma_start(patch[PL:PL + 1, :, :], b_in.rearrange("(a c d) -> a c d", a=1, c=1).broadcast_to([1, B, D])).then_inc(ld["bin"], 16)

            act.wait_ge(ld["ctx"], 16)
            for b in range(B):
                if b:
                    act.wait_ge(s_ctxss, b)
                nc.scalar.activation(ctx_sq[:], ctx_sb[:, b, :], ACT.Square, accum_out=ctx_ss[:, b:b + 1]).then_inc(s_ctxss, 1)
            act.wait_ge(ld["slots"], 16)
            for j in range(ET):
                if j:
                    act.wait_ge(s_slotss, j)
                nc.scalar.activation(slot_sq[:], slot_raw[:, j, :], ACT.Square, accum_out=slot_ss[:, j:j + 1]).then_inc(s_slotss, 1)
            act.wait_ge(ld["small"], 16)
            nc.scalar.activation(tanh_g[:], cst[:, C_GATES:C_GATES + 2], ACT.Tanh).then_inc(s_tanh, 1)

            def copy_out(u, dst, bank):
                act.wait_ge(t_done, u + 1)
                nc.scalar.activation(dst, pT[bank][:].rearrange("p (t q) -> p t q", q=P), ACT.Copy).then_inc(t_out, 1)

            def out_hT(c, use):
                act.wait_ge(a2_done, c)
                copy_out(use[0], hT[:], use[1])

            def out_zT(use):
                copy_out(use[0], zT_hi[:], use[1])

            def exp_C(b, i):
                act.wait_ge(max_done, 4 * b + i + 1)
                nc.scalar.activation(C[:, i, :], pL[i][:], ACT.Exp, bias=nmC[:, i:i + 1], accum_out=sumC[:, i:i + 1]).then_inc(expC_done, 1)

            def exp_D(b, i):
                if i == 0:
                    act.wait_ge(shifted0, b + 1)
                else:
                    act.wait_ge(shifted, (NT - 1) * b + i)
                nc.scalar.activation(Dn[:, i, :], Dn[:, i, :], ACT.Exp).then_inc(expD_done, 1)

            def out_C(b, i, after):
                u, bank = t_C(b, i, after)
                copy_out(u, CT[:, b, :, i * P:(i + 1) * P], bank)

            def keep_logits0(b):
                act.wait_ge(max_done, 4 * b + 1)
                nc.scalar.activation(logits0[:], pL[0][:], ACT.Copy).then_inc(logits0_kept, 1)

            def out_rows(b):
                act.wait_ge(nmT_done, b + 1)
                nc.scalar.activation(nm_rows[:], pR[:], ACT.Copy).then_inc(nm_rows_ready, 1)

            def out_slotsT(b):
                act.wait_ge(slotsT_done, b + 1)
                nc.scalar.activation(slotsT_hi[:, :, b, :], pM[:].rearrange("p (e s) -> p e s", e=E), ACT.Copy,
                                     scale=cols[:, V_NG:V_NG + 1]).then_inc(slotsT_hi_ready, 1)

            def all_of_slotsT(b):
                if not isinstance(b, int) or b:
                    act.wait_ge(slotsT_split, b)
                nc.scalar.activation(slotsT[:], pM[:].rearrange("p (e s) -> p e s", e=E), ACT.Copy,
                                     scale=cols[:, V_NG:V_NG + 1]).then_inc(slotsT_ready, 1)

            def tokens_softmax(c, after, slots_of=None):
                out_C(c, 1, after)
                if after:
                    out_zT(t_zT(c + 1))
                exp_C(c, 2)
                exp_C(c, 3)
                out_rows(c)
                if slots_of is not None:
                    out_slotsT(slots_of)
                    all_of_slotsT(slots_of)
                if after:
                    out_C(c, 2, after)

            def split_w1(b, k):
                act.wait_ge(ld_w, 16 * 2 * E)
                nc.scalar.activation(w1_hi[:, 2 * b + k, :], w1_sb[:, 2 * b + k, :], ACT.Copy).then_inc(w_hi_ready, 1)

            def turn(b, after):
                if after > 1:
                    out_hT(b + 2, t_hT(b + 2))
                if after > 1:
                    split_w1(b, 0)
                if after:
                    out_C(b, NT - 1, after)
                exp_D(b, 0)
                if after:
                    keep_logits0(b + 1)
                    exp_C(b + 1, 0)
                exp_D(b, 1)
                exp_D(b, 2)
                exp_D(b, 3)
                if not after:
                    out_C(b, 2, 0)
                    out_C(b, NT - 1, 0)
                if after <= 1:
                    split_w1(b, 0)
                split_w1(b, 1)
                if after:
                    exp_C(b + 1, 1)
                    out_C(b + 1, 0, after - 1)
                    tokens_softmax(b + 1, after - 1, b)
                else:
                    nc.scalar.activation(gelu_try[:], half_neg[:, 0:1], ACT.Gelu)
                    for k, (e0, e1, src) in enumerate(((0, FE, pL[2][:, 0:P]), (FE, E, pL[3][:, P:]))):
                        act.wait_ge(slotsT_done, b + 1 + k)
                        nc.scalar.activation(slotsT_hi[:, e0:e1, b, :], src.rearrange("p (e s) -> p e s", s=S), ACT.Copy,
                                             scale=cols[:, V_NG:V_NG + 1]).then_inc(slotsT_hi_ready, 1)

            copy_out(0, hT[:], 0)
            act.wait_ge(s_count, 1)
            for b in range(B):
                if b == 1:
                    act.wait_ge(s_depp, 1)
                    nc.scalar.activation(depool[:, 0, :], pL[3][0:PL + 1, 0:D], ACT.Copy).then_inc(s_dep0, 1)
                nc.scalar.activation(plug_blk[:, b, :], count, ACT.Relu, scale=cst[0:B, C_SEL + b:C_SEL + b + 1]).then_inc(s_plug, 1)
            act.wait_ge(s_depp, 2)
            nc.scalar.activation(depool[:, 1:, :], pL[3][0:PL + 1, D:].rearrange("p (b d) -> p b d", d=D), ACT.Copy).then_inc(s_dep, 1)
            out_hT(1, (1, 1))
            act.wait_ge(s_gg, 1)
            act.wait_ge(s_snTp, 1)
            nc.scalar.activation(snT[:], pL[2][:], ACT.Copy, scale=gn_gs[:, 0:1]).then_inc(s_snT, 1)
            act.wait_ge(s_snT, 1)
            nc.scalar.activation(snT_hi[:], snT[:], ACT.Copy).then_inc(s_snT, 1)
            out_zT((2, 0))
            keep_logits0(0)
            exp_C(0, 0)
            exp_C(0, 1)
            out_C(0, 0, 2)
            act.wait_ge(s_cols, 1)
            tokens_softmax(0, 2)
            with act.Fori(0, B - 2) as b:
                turn(b, 2)
            turn(B - 2, 1)
            turn(B - 1, 0)

            for e in range(E):
                if e >= 2:
                    act.wait_ge(eoT_done, e - 1)
                for j in range(HT):
                    k = e * HT + j
                    act.wait_ge(h_done, k // 2 + 1)
                    nc.scalar.activation(h[:, e % 2, j, :], pL[(k // 2) % 4][:, (k % 2) * BS:(k % 2 + 1) * BS],
                                         ACT.Gelu, bias=cols[:, k:k + 1]).then_inc(gelu_done, 1)

        @block.vector
        def _(dve):
            steps = [0]

            def step(ins):
                steps[0] += 1
                ins.then_inc(s_dve, 1)
                dve.wait_ge(s_dve, steps[0])

            def mean_var1(b):
                dve.wait_ge(ld_x[b], 16)
                for t in range(NT):
                    last = nc.vector.bn_stats(stats1[:, b * NT + t, :], x_sb[:, b, t * D:(t + 1) * D])
                step(last)
                for t in range(NT):
                    last = nc.vector.bn_aggr(mv1[:, b * NT + t, :], stats1[:, b * NT + t, :])
                step(last)

            def shift_var1(b0, b1_):
                return nc.vector.tensor_scalar(var1[:, b0 * NT:b1_ * NT], mv1[:, b0 * NT:b1_ * NT, 1], NORM1_SHIFT, None, ALU.add)

            def make_onehot(c):
                dve.wait_ge(bc_done, c + 1)
                nc.vector.tensor_scalar(onehot[:], pR[0:PL + 1, :], cst[0:PL + 1, C_Q:C_Q + 1], None, ALU.is_equal).then_inc(onehot_ready, 1)

            def residual1(c):
                dve.wait_ge(a2_done, c + 1)
                nc.vector.scalar_tensor_tensor(x1[:, c, :], pM[:], tanh_g[:, 0:1], x_sb[:, c, :], ALU.mult, ALU.add).then_inc(x1_ready, 1)

            def stats_of_x1(c):
                for t in range(NT):
                    last = nc.vector.bn_stats(stats2[:, t, :], x1[:, c, t * D:(t + 1) * D])
                return last.then_inc(stats2_ready, 1)

            def aggregate():
                for t in range(NT):
                    last = nc.vector.bn_aggr(mv2[:, t, :], stats2[:, t, :])
                last.then_inc(mv2_ready, 1)

            def clamp_var2(c, link):
                dve.wait_ge(mv2_ready, c + 1)
                k = NORM_FLOOR ** 2 / D
                link(nc.vector.tensor_scalar(floor2[:], mv2[:, :, 1], LN_EPS, k, ALU.add, ALU.mult))
                nc.vector.tensor_tensor(var2[:], mv2[:, :, 1], floor2[:], ALU.max).then_inc(var2_ready, 1)

            def zT_rest(use):
                dve.wait_ge(t_out, use[0] + 1)
                nc.vector.tensor_tensor(zT_lo[:].rearrange("d t q -> d (t q)"), pT[use[1]][:],
                                        zT_hi[:].bitcast(F32).rearrange("d t q -> d (t q)"), ALU.subtract).then_inc(zlo_ready, 1)

            def norm2(c, tiles):
                dve.wait_ge(c2_ready, c + 1)
                if not isinstance(c, int) or c:
                    dve.wait_ge(zs_ready, c)
                for t in range(tiles):
                    last = nc.vector.tensor_scalar(z[:, t, :], x1[:, c, t * D:(t + 1) * D], mv2[:, t, 0:1], c2[:, t:t + 1],
                                                   ALU.subtract, ALU.mult)
                return last

            def norm1(c):
                for t in range(NT):
                    last = nc.vector.tensor_scalar(z1[:, t, :], x_sb[:, c, t * D:(t + 1) * D], mv1[:, c * NT + t, 0:1],
                                                   c1[:, bass.ds(c * NT + t, 1)], ALU.subtract, ALU.mult)
                last.then_inc(z1_ready, 1)

            def scale_patches(b0, b1_):
                for b in range(b0, b1_):
                    last = nc.vector.scalar_tensor_tensor(patch[0:PL, b, :], ctx_sb[:, b, 0:D], rms[0:PL, b:b + 1],
                                                          cst[0:PL, C_GINIT:C_GINIT + D], ALU.mult, ALU.mult)
                last.then_inc(s_patch, 1)

            nc.vector.memset(warm[:], 0.0).then_inc(s_warm, 1)
            mean_var1(0)
            shift_var1(0, 1).then_inc(s_var1, 1)

            dve.wait_ge(s_cum, 1)
            step(nc.vector.tensor_scalar(bound_w[:], pR[0:PL, 0:B], 1.0, float(N), ALU.is_lt, ALU.mult))
            step(nc.vector.scalar_tensor_tensor(bound[:], pR[0:PL, 0:B], -1.0, bound_w[:], ALU.add, ALU.add))
            dve.wait_ge(s_iota, 1)
            for b in range(B):
                nc.vector.tensor_scalar(hits[:, b, :], iota, bound[:, b:b + 1], None, ALU.is_equal).then_inc(s_hits, 1)
            dve.wait_ge(s_ms, 1)
            dve.wait_ge(s_ctxss, 1)
            nc.vector.tensor_scalar(ms[0:PL, 0:1], ctx_ss[:, 0:1], 1.0 / DG, RMS_EPS, ALU.mult, ALU.add).then_inc(s_ms0, 1)
            dve.wait_ge(s_c1, 1)
            norm1(0)
            dve.wait_ge(s_colsp, 1)
            nc.vector.tensor_copy(cols[:], pL[0][:, 0:VROWS]).then_inc(s_cols, 1)
            dve.wait_ge(s_rms, 1)
            scale_patches(0, 1)
            dve.wait_ge(s_cnt, 1)
            step(nc.vector.tensor_scalar(bound_row, pR[0:B, :], 1.0, None, ALU.min))
            dve.wait_ge(s_cap, 1)
            nc.vector.tensor_tensor_scan(count, bound_row, cap, -1.0, ALU.add, ALU.min).then_inc(s_count, 1)
            dve.wait_ge(s_cols, 1)
            dve.wait_ge(s_WTp, 1)
            nc.vector.tensor_scalar(WT[:], pL[1][:, 0:D], cols[:, V_GRES:V_GRES + 1], NORM1_GAIN, ALU.mult, ALU.mult).then_inc(s_WT, 1)
            dve.wait_ge(s_ctxss, B)
            dve.wait_ge(s_slotss, ET)
            nc.vector.tensor_scalar(ms[0:PL, 1:B], ctx_ss[:, 1:B], 1.0 / DG, RMS_EPS, ALU.mult, ALU.add)
            nc.vector.tensor_scalar(ms[:, B:], slot_ss[:], NORM_FLOOR ** 2, 1.0 / D, ALU.max, ALU.mult).then_inc(s_msr, 1)
            make_onehot(0)
            mean_var1(1)
            shift_var1(1, 2).then_inc(s_var1, 1)
            dve.wait_ge(s_rms, 2)
            scale_patches(1, B)
            dve.wait_ge(s_tanh, 1)
            residual1(0)
            dve.wait_ge(x1_ready, 1)
            stats_of_x1(0)
            dve.wait_ge(stats2_ready, 1)
            aggregate()
            clamp_var2(0, step)
            for j in range(ET):
                last = nc.vector.tensor_scalar(slot_n[:, j, :], slot_raw[:, j, :], rms[:, B + j:B + j + 1], None, ALU.mult)
            last.then_inc(s_slotn, 1)
            nc.vector.tensor_tensor(gn_gs[:], cols[:, V_NG:V_NG + 1], cols[:, V_SG:V_SG + 1], ALU.mult).then_inc(s_gg, 1)
            norm2(0, NT).then_inc(z_ready, 1)
            make_onehot(1)
            dve.wait_ge(s_snT, 2)
            nc.vector.tensor_tensor(snT_lo[:], snT[:], snT_hi[:].bitcast(F32), ALU.subtract).then_inc(snlo_ready, 1)
            zT_rest((2, 0))
            mean_var1(2)
            shift_var1(2, 3).then_inc(s_var1, 1)

            def token_max(b, i):
                dve.wait_ge(logits_done, 4 * b + i + 1)
                return nc.vector.tensor_reduce(nmC[:, i:i + 1], pL[i][:], AX.X, ALU.max, negate=True)

            def slot_max(b, i):
                if i == 1:
                    dve.wait_ge(logits0_kept, b + 1)
                else:
                    dve.wait_ge(max_done, 4 * b + i)
                return nc.vector.tensor_tensor(cmax[:], logits0[:] if i == 1 else cmax[:], pL[i][:], ALU.max).then_inc(max_done, 1)

            def reduce_slot_max(b):
                dve.wait_ge(cmaxT_done, b + 1)
                nc.vector.tensor_reduce(nmD[:], pR[:].rearrange("p (j n) -> p j n", n=P), AX.X, ALU.max, negate=True).then_inc(nm_ready, 1)

            def shift(b, i):
                dve.wait_ge(nm_rows_ready, b + 1)
                nc.vector.tensor_tensor(Dn[:, i, :], pL[i][:], nm_rows[:], ALU.add).then_inc(shifted, 1)

            residual1(1)
            token_max(0, 0).then_inc(max_done, 1)
            dve.wait_ge(x1_ready, 2)
            stats_of_x1(1)
            dve.wait_ge(stats2_ready, 2)
            aggregate()
            clamp_var2(1, step)
            token_max(0, 1)
            slot_max(0, 1)
            token_max(0, 2)
            norm2(1, HALF).then_inc(z_ready, 1)
            slot_max(0, 2)
            token_max(0, 3)
            slot_max(0, 3)
            reduce_slot_max(0)
            zT_rest(t_zT(1))
            mean_var1(3)
            shift_var1(3, B).then_inc(s_var1, 1)

            base = steps[0]
            LINKS = (1, 1, 2)

            def turn(b, before, after):
                links = [0]

                def link(ins):
                    links[0] += 1
                    ins.then_inc(s_dve, 1)
                    dve.wait_ge(s_dve, before + links[0])

                dve.wait_ge(expC_done, 4 * b + NT)
                nc.vector.reciprocal(rC[:, b, :], sumC[:]).then_inc(rC_ready, 1)
                if after:
                    token_max(b + 1, 0).then_inc(max_done, 1)
                if not after:
                    dve.wait_ge(nm_rows_ready, b + 1)
                    nc.vector.tensor_tensor(Dn[:, 0, :], logits0[:], nm_rows[:], ALU.add).then_inc(shifted0, 1)
                shift(b, 1)
                if after > 1:
                    make_onehot(b + 2)
                shift(b, 2)
                shift(b, 3)
                if after:
                    token_max(b + 1, 1)
                    slot_max(b + 1, 1)
                if after > 1:
                    residual1(b + 2)
                    dve.wait_ge(x1_ready, b + 3)
                if after:
                    token_max(b + 1, 2)
                if after > 1:
                    stats_of_x1(b + 2)
                    dve.wait_ge(stats2_ready, b + 3)
                if after:
                    slot_max(b + 1, 2)
                if after > 1:
                    aggregate()
                    clamp_var2(b + 2, link)
                if after:
                    token_max(b + 1, 3)
                dve.wait_ge(slots_done, b + 1)
                nc.vector.reciprocal(rD[:, 0:ET - 1], pM[:, 0:(ET - 1) * (D + 1)].rearrange("p (j d) -> p j d", d=D + 1)[:, :, D])
                link(nc.vector.reciprocal(rD[:, ET - 1:], pR[:, D:D + 1]))
                first = 0
                if not after:
                    first = 1
                    nc.vector.tensor_scalar(slots_sb[:, 0, :], pM[:, 0:D], rD[:, 0:1], None, ALU.mult).then_inc(slots_out, 1)
                nc.vector.tensor_scalar(slots_sb[:, ET - 1, :], pR[:, 0:D], rD[:, ET - 1:], None, ALU.mult)
                if after > 1:
                    norm2(b + 2, HALF).then_inc(z_ready, 1)
                if after:
                    slot_max(b + 1, 3)
                nc.vector.tensor_tensor(slots_sb[:, first:ET - 1, :], pM[:, first * (D + 1):(ET - 1) * (D + 1)].rearrange("p (j d) -> p j d", d=D + 1)[:, :, 0:D],
                                        rD[:, first:ET - 1].rearrange("p (j a) -> p j a", a=1).broadcast_to([P, ET - 1 - first, D]), ALU.mult).then_inc(slots_out, 1)
                if after:
                    reduce_slot_max(b + 1)
                if after > 1:
                    zT_rest(t_zT(b + 2))
                assert links[0] == LINKS[after], links

            with dve.Fori(0, B - 2) as b:
                turn(b, base + LINKS[2] * b, 2)
            turn(B - 2, base + LINKS[2] * (B - 2), 1)
            turn(B - 1, base + LINKS[2] * (B - 2) + LINKS[1], 0)

            for k, (e0, e1, src) in enumerate(((0, FE, pL[2][:, 0:P]), (FE, E, pL[3][:, P:]))):
                dve.wait_ge(slotsT_hi_ready, B + k)
                nc.vector.scalar_tensor_tensor(slotsT_lo[:, e0:e1, B - 1, :], src.rearrange("p (e s) -> p e s", s=S), cols[:, V_NG:V_NG + 1],
                                               slotsT_hi[:, e0:e1, B - 1, :].bitcast(F32), ALU.mult, ALU.subtract).then_inc(slotsT_lo_last, 1)

            dve.wait_ge(rC_ready, B)
            nc.vector.tensor_scalar(scC[:], rC[:], tanh_g[:, 1:2], None, ALU.mult).then_inc(sc_ready, 1)
            dve.wait_ge(sc_ready, 1)

            def out_eo(i):
                dve.wait_ge(eo_done, i + 1)
                nc.vector.tensor_copy(eo[:, i, :, :], pT[i % 2][:].rearrange("p (b d) -> p b d", b=B)).then_inc(eo_ready, 1)

            for e in range(E):
                if e >= 3 and e % 2:
                    out_eo((e - 3) // 2)
                dve.wait_ge(eoT_done, e + 1)
                bank = pM if e % 2 == 0 else pR
                nc.vector.tensor_scalar(eoT[:, :, e * S:(e + 1) * S], bank[:, 0:BS].rearrange("p (b s) -> p b s", b=B),
                                        cols[:, V_B2 + e:V_B2 + e + 1], None, ALU.add).then_inc(eoT_ready, 1)
            out_eo(ET - 1)

            def residual2(b, t, src):
                return nc.vector.scalar_tensor_tensor(y_sb[:, b, t * D:(t + 1) * D], src, scC[:, b, t:t + 1],
                                                      x1[:, b, t * D:(t + 1) * D], ALU.mult, ALU.add)

            for b in range(B - 1):
                dve.wait_ge(y_done, b + 1)
                for t in range(NT):
                    last = residual2(b, t, pL[b][:, t * D:(t + 1) * D])
                last.then_inc(y_ready, 1)
            for t in range(NT):
                dve.wait_ge(y_tile_done, t + 1)
                residual2(B - 1, t, last_banks[t][:, 0:D]).then_inc(y_tile_ready, 1)

        @block.tensor
        def _(pe):
            mm = nc.tensor.matmul

            def keep_warm(bank, n):
                for _ in range(n):
                    mm(bank[:], warm[:, 0:P], warm[:], start=True, stop=True)

            pe.wait_ge(ld["small"], 16)
            pe.wait_ge(s_lensf, 1)
            mm(pR[0:PL, 0:B], cst[0:PL, C_TRI:C_TRI + PL], lens_f[:], start=True, stop=True).then_inc(s_cum, 1)
            nc.tensor.transpose(pL[0][:, 0:VROWS], cst[0:VROWS, C_ROWS:C_ROWS + D], cst[0:VROWS, C_ID:C_ID + VROWS]).then_inc(s_colsp, 1)
            pe.wait_ge(ld["W"], 16)
            nc.tensor.transpose(pL[1][:, 0:D], W_sb[:], ident).then_inc(s_WTp, 1)

            def transposes(u, bank, srcs, free):
                if free:
                    pe.wait_ge(t_out, u - 1)
                for k, src in enumerate(srcs):
                    last = nc.tensor.transpose(pT[bank][:, k * P:(k + 1) * P], src, ident)
                last.then_inc(t_done, 1)

            def tr_hT(c, use, free=True):
                pe.wait_ge(z1_ready, c + 1)
                transposes(*use, [z1[:, t, :] for t in range(NT)], free)

            def tr_zT(c, use, free=True):
                pe.wait_ge(z_ready, c + 1)
                if not isinstance(c, int) or c:
                    pe.wait_ge(zp_ready, c)
                transposes(*use, [z[:, t, :] for t in range(NT)], free)

            def spread_plug(c):
                mm(pR[0:PL + 1, :], ones_bf[:], plug_blk[:, c, :].rearrange("b (p t) -> b t p", t=NT), start=True, stop=True).then_inc(bc_done, 1)

            def residual_W(c, tiles=range(NT)):
                pe.wait_ge(t_out, (t_hT(c) if not isinstance(c, int) or c > 1 else (c, c))[0] + 1)
                for t in tiles:
                    mm(pM[:, t * D:(t + 1) * D], hT[:, t, :], WT[:], start=(t == 0), stop=False)

            def residual_depool(c):
                pe.wait_ge(onehot_ready, c + 1)
                for t in range(NT):
                    last = mm(pM[:, t * D:(t + 1) * D], onehot[:, t * P:(t + 1) * P], depool[:, c, :], start=False, stop=(t == NT - 1))
                last.then_inc(a2_done, 1)

            def logits(b, i):
                if i and not (isinstance(b, int) and b == 0):
                    pe.wait_ge(shifted, (NT - 1) * (b - 1) + i)
                for n, (a, c) in enumerate(((zT_hi, snT_hi), (zT_lo, snT_hi), (zT_hi, snT_lo))):
                    last = mm(pL[i][:], a[:, i, :], c[:], start=(n == 0), stop=(n == 2))
                last.then_inc(logits_done, 1)

            pe.wait_ge(s_bf, 3)
            for b in range(B):
                pe.wait_ge(s_hits, b + 1)
                last = mm(pR[0:B, :], blk_bf[:, b, :], hits[:, b, :], start=(b == 0), stop=(b == B - 1))
            last.then_inc(s_cnt, 1)
            tr_hT(0, (0, 0), False)
            pe.wait_ge(ld["bin"], 16)
            pe.wait_ge(s_patch, 1)
            mm(pL[3][0:PL + 1, 0:D], cst[0:PL + 1, C_DEC:C_DEC + PL + 1], patch[:, 0, :], start=True, stop=True).then_inc(s_depp, 1)
            pe.wait_ge(s_WT, 1)
            residual_W(0, range(HALF))
            pe.wait_ge(s_plug, 1)
            spread_plug(0)
            residual_W(0, range(HALF, NT))
            pe.wait_ge(s_dep0, 1)
            residual_depool(0)
            pe.wait_ge(s_warm, 1)
            keep_warm(pL[1], 1)
            pe.wait_ge(s_patch, 2)
            mm(pL[3][0:PL + 1, D:], cst[0:PL + 1, C_DEC:C_DEC + PL + 1], patch[:, 1:, :].rearrange("p b d -> p (b d)"), start=True, stop=True).then_inc(s_depp, 1)
            keep_warm(pL[1], 2)
            tr_hT(1, (1, 1), False)
            pe.wait_ge(s_slotn, 1)
            for j in range(ET):
                last = nc.tensor.transpose(pL[2][:, j * P:(j + 1) * P], slot_n[:, j, :], ident)
            last.then_inc(s_snTp, 1)
            pe.wait_ge(s_plug, B)
            spread_plug(1)
            tr_zT(0, (2, 0))
            pe.wait_ge(x1_ready, 1)
            residual_W(1)
            pe.wait_ge(s_dep, 1)
            residual_depool(1)
            pe.wait_ge(snlo_ready, 1)

            def tr_C(b, i, after):
                pe.wait_ge(expC_done, 4 * b + i + 1)
                transposes(*t_C(b, i, after), [C[:, i, j * P:(j + 1) * P] for j in range(ET)], True)

            def tr_cmax(b):
                pe.wait_ge(max_done, 4 * b + NT)
                for j in range(ET):
                    last = nc.tensor.transpose(pR[:, j * P:(j + 1) * P], cmax[:, j * P:(j + 1) * P], ident)
                last.then_inc(cmaxT_done, 1)

            def tr_nm(b):
                pe.wait_ge(nm_ready, b + 1)
                for j in range(ET):
                    last = nc.tensor.transpose(pR[:, j * P:(j + 1) * P], nmD[:, j:j + 1].broadcast_to([P, P]), ident)
                last.then_inc(nmT_done, 1)

            def maxima_and_C(c, after, slots_before=None):
                tr_C(c, 1, after)
                if after:
                    tr_zT(c + 1, t_zT(c + 1))
                tr_cmax(c)
                if slots_before is not None:
                    slots_before()
                tr_nm(c)
                if after:
                    pe.wait_ge(zlo_ready, c + 2)
                    logits(c + 1, 0)
                tr_C(c, 2, after)

            pe.wait_ge(zlo_ready, 1)
            for i in range(NT):
                logits(0, i)
            keep_warm(pT[1], 3)
            pe.wait_ge(s_ones, 1)

            tr_C(0, 0, 2)
            maxima_and_C(0, 2)

            def turn(b, after):
                def slots(t):
                    pe.wait_ge(expD_done, 4 * b + t + 1)
                    for j in range(ET):
                        dst = pM[:, j * (D + 1):(j + 1) * (D + 1)] if j < ET - 1 else pR[:, 0:D + 1]
                        last = mm(dst, Dn[:, t, j * P:(j + 1) * P], zs[:, b, t, :],
                                  start=(t == 0 and j in (0, ET - 1)), stop=(t == NT - 1 and j >= ET - 2))
                    return last

                def tr_slots():
                    pe.wait_ge(slots_out, b + 1)
                    for j in range(ET):
                        last = nc.tensor.transpose(pM[:, j * P:(j + 1) * P], slots_sb[:, j, :], ident)
                    last.then_inc(slotsT_done, 1)

                if after > 1:
                    pe.wait_ge(nm_rows_ready, b + 1)
                    spread_plug(b + 2)
                    tr_hT(b + 2, t_hT(b + 2))
                tr_C(b, NT - 1, after)
                if after:
                    logits(b + 1, 1)
                if after > 1:
                    residual_W(b + 2)
                    residual_depool(b + 2)
                if after:
                    logits(b + 1, 2)
                    logits(b + 1, 3)
                if not after:
                    keep_warm(pL[0], 8)
                pe.wait_ge(zs_ready, b + 1)
                if after > 1:
                    pe.wait_ge(x1_ready, b + 3)
                else:
                    pe.wait_ge(slotsT_ready, b)
                slots(0)
                slots(1)
                slots(2)
                slots(3).then_inc(slots_done, 1)
                if after:
                    tr_C(b + 1, 0, after - 1)
                    maxima_and_C(b + 1, after - 1, tr_slots)
                else:
                    keep_warm(pL[0], 4)
                    pe.wait_ge(slots_out, b + 1)
                    nc.tensor.transpose(pL[2][:, 0:P], slots_sb[:, 0, :], ident).then_inc(slotsT_done, 1)
                    pe.wait_ge(slots_out, b + 2)
                    for j in range(1, ET):
                        last = nc.tensor.transpose(pL[3][:, j * P:(j + 1) * P], slots_sb[:, j, :], ident)
                    last.then_inc(slotsT_done, 1)

            with pe.Fori(0, B - 2) as b:
                turn(b, 2)
            turn(B - 2, 1)
            turn(B - 1, 0)

            def hidden(e):
                pe.wait_ge(w_lo_ready, e + 1)

                def product(j, n):
                    k = e * HT + j
                    a, c = ((w1_hi, slotsT_hi), (w1_lo, slotsT_hi), (w1_hi, slotsT_lo))[n]
                    return mm(pL[(k // 2) % 4][:, (k % 2) * BS:(k % 2 + 1) * BS], a[:, e, j * P:(j + 1) * P],
                              c[:, e, :, :].rearrange("d b s -> d (b s)"), start=(n == 0 and k % 2 == 0), stop=(n == 2 and k % 2 == 1))

                if e == 1:
                    pe.wait_ge(slotsT_hi_ready, B + 1)
                    pe.wait_ge(slotsT_lo_last, 2)
                if e == 0:
                    for j in range(HT):
                        product(j, 0)
                        product(j, 1)
                    pe.wait_ge(slotsT_split, B - 1)
                    pe.wait_ge(slotsT_lo_last, 1)
                for j in range(HT):
                    k = e * HT + j
                    if k % 2 == 0 and k >= 8:
                        pe.wait_ge(gelu_done, k - 6)
                    for n in ([2] if e == 0 else range(3)):
                        last = product(j, n)
                    if k % 2:
                        last.then_inc(h_done, 1)

            def down(e):
                pe.wait_ge(gelu_done, HT * (e + 1))
                bank = pM if e % 2 == 0 else pR
                if e >= 2:
                    pe.wait_ge(eoT_ready, e - 1)
                for j in range(HT):
                    last = mm(bank[:, 0:BS], w2_sb[:, e, j, :], h[:, e % 2, j, :], start=(j == 0), stop=(j == HT - 1))
                last.then_inc(eoT_done, 1)

            def tr_eo(i):
                pe.wait_ge(eoT_ready, 2 * i + 2)
                if i >= 2:
                    pe.wait_ge(eo_ready, i - 1)
                for b in range(B):
                    last = nc.tensor.transpose(pT[i % 2][:, b * P:(b + 1) * P], eoT[:, b, i * P:(i + 1) * P], ident)
                last.then_inc(eo_done, 1)

            pe.wait_ge(slotsT_hi_ready, B)
            hidden(0)
            pe.wait_ge(t_out, EARLIER_USES)
            for e in range(E):
                if e + 1 < E:
                    hidden(e + 1)
                if e >= 2 and e % 2 == 0:
                    tr_eo(e // 2 - 1)
                down(e)
            def y_part(b, tiles):
                for i in tiles:
                    pe.wait_ge(eo_ready, i + 1)
                    for t in range(NT):
                        last = mm(pL[b][:, t * D:(t + 1) * D], CT[:, b, i, t * P:(t + 1) * P], eo[:, i, b, :],
                                  start=(i == 0 and t == 0), stop=(i == ET - 1 and t == NT - 1))
                return last

            pe.wait_ge(gelu_done, E * HT)
            y_part(0, range(ET - 1))
            tr_eo(ET - 1)
            y_part(1, range(ET - 1))
            y_part(0, [ET - 1]).then_inc(y_done, 1)
            y_part(1, [ET - 1]).then_inc(y_done, 1)
            for b in range(2, B - 1):
                y_part(b, range(ET)).then_inc(y_done, 1)
            for t in range(NT):
                for i in range(ET):
                    last = mm(last_banks[t][:, 0:D], CT[:, B - 1, i, t * P:(t + 1) * P], eo[:, i, B - 1, :], start=(i == 0), stop=(i == ET - 1))
                last.then_inc(y_tile_done, 1)



_INS = ['x', 'ctx_2048', 'mask_BxS2_if0', 'L0_xattn_W_in', 'L0_xattn_b_in', 'L0_ffn_slot_embeds', 'L0_ffn_w1',
        'L0_ffn_w2', 'small']


def kernel(**inputs):
    import numpy as _np
    import concourse.bacc as _bacc
    from concourse import mybir as _mybir
    from concourse.bass_utils import run_bass_kernel_spmd as _run

    given = {k: _np.asarray(v) for k, v in inputs.items()}
    given['mask_BxS2_if0'] = given['mask_BxS2_if0'].T
    small = shape_constants()
    rows = [given['L0_ffn_b1'].reshape(E * HT, D), given['L0_ffn_b2'], given['L0_xattn_g_res'].reshape(1, D),
            given['L0_ffn_norm_gamma'].reshape(1, D), given['L0_ffn_slot_norm_gamma'].reshape(1, D)]
    small[:VROWS, C_ROWS:C_ROWS + D] = _np.concatenate(rows)
    small[:, C_GINIT:C_GINIT + D] = given['L0_xattn_g_init'][:D]
    small[:, C_GATES] = given['g_xattn']
    small[:, C_GATES + 1] = given['g_ffn']
    given['small'] = small

    nc = _bacc.Bacc("TRN2", target_bir_lowering=False, num_devices=1)
    arrays, args = {}, []
    for name in _INS:
        a = _np.ascontiguousarray(given[name])
        arrays[f"in_{name}"] = a
        args.append(nc.dram_tensor(f"in_{name}", a.shape, _mybir.dt.from_np(a.dtype), kind="ExternalInput").ap())
    y = nc.dram_tensor("out_y", (B, N, D), F32, kind="ExternalOutput").ap()
    flamingo_kernel(nc, *args, y)
    r = _run(nc, [arrays], core_ids=[0])
    return r.results[0]["out_y"]
```
